# Optimizing a Trainium2 kernel written in Bass

```python
import numpy as np
import jax
import jax.numpy as jnp

def _softmax(x, axis=-1):
    return jax.nn.softmax(x, axis=axis)

def _gelu(x):
    return jax.nn.gelu(x, approximate=True)

def _silu(x):
    return jax.nn.silu(x)

def _sigmoid(x):
    return jax.nn.sigmoid(x)

def _layernorm(x, axis=-1, eps=1e-05):
    m = jnp.mean(x, axis=axis, keepdims=True)
    v = jnp.var(x, axis=axis, keepdims=True)
    return (x - m) / jnp.sqrt(v + eps)

def _scatter_add(tgt, idx, src, axis=0):
    return tgt.at[idx].add(src)

def _segment_sum(src, seg, n):
    return jax.ops.segment_sum(src, seg, n)
kernel_name = 'mk_gps_d1_gnn_r8_aad0cd'

def setup_inputs(seed: int=0):
    np.random.seed(seed)
    _w = jnp.asarray

    def _rec_inputs():
        import jax
        import jax.numpy as jnp
        _gk = jax.random.key(seed)
        x = -0.000364 + 1 * jax.random.normal(jax.random.fold_in(_gk, 1), (1250, 768), jnp.float32)
        _s = jax.random.randint(jax.random.fold_in(_gk, 2), (20000,), 0, 1250, jnp.int32)
        _d = jax.random.randint(jax.random.fold_in(_gk, 3), (20000,), 0, 1250, jnp.int32)
        _loop = jnp.arange(1250, dtype=jnp.int32)
        src = jnp.concatenate([_s, _d, _loop])
        dst = jnp.concatenate([_d, _s, _loop])
        _o = jnp.argsort(dst, stable=True)
        src = src[_o]
        dst = dst[_o]
        edge_type_8 = jax.random.randint(jax.random.fold_in(_gk, 12), (41250,), 0, 8, jnp.int32)
        return (x, src, dst, edge_type_8)
    x, src, dst, edge_type_8 = _rec_inputs()

    def _L0_gnn_setup():
        import jax, jax.numpy as jnp
        import numpy as np
        N, IN, OUT, R, E = (2500, 768, 768, 8, 40000)

        def _rgcn_conv(x, src, dst, etype, W, root, b):
            num_nodes = x.shape[0]
            num_rel = W.shape[0]
            x_src = x[src]
            seg = dst * num_rel + etype
            sums = jax.ops.segment_sum(x_src, seg, num_segments=num_nodes * num_rel)
            cnt = jax.ops.segment_sum(jnp.ones((src.shape[0],), dtype=x.dtype), seg, num_segments=num_nodes * num_rel)
            mean = sums / jnp.maximum(cnt, 1.0)[:, None]
            mean = mean.reshape(num_nodes, num_rel, -1)
            out = jnp.einsum('nri,rio->no', mean, W)
            return out + x @ root + b
        key = jax.random.key(seed)
        ks = jax.random.split(key, 9)
        x = jax.random.normal(ks[0], (N, IN), dtype=jnp.float32)
        edge_index = jax.random.randint(ks[1], (2, E), 0, N, dtype=jnp.int64)
        edge_type = jax.random.randint(ks[2], (E,), 0, R, dtype=jnp.int64)
        s1 = 1.0 / np.sqrt(IN)
        s2 = 1.0 / np.sqrt(OUT)
        W1 = jax.random.normal(ks[3], (R, IN, OUT), dtype=jnp.float32) * s1
        root1 = jax.random.normal(ks[4], (IN, OUT), dtype=jnp.float32) * s1
        b1 = jnp.zeros((OUT,), dtype=jnp.float32)
        W2 = jax.random.normal(ks[5], (R, OUT, OUT), dtype=jnp.float32) * s2
        root2 = jax.random.normal(ks[6], (OUT, OUT), dtype=jnp.float32) * s2
        b2 = jnp.zeros((OUT,), dtype=jnp.float32)
        return {'x': x, 'edge_index': edge_index, 'edge_type': edge_type, 'W1': W1, 'root1': root1, 'b1': b1, 'W2': W2, 'root2': root2, 'b2': b2}
    _L0_gnn_all = _L0_gnn_setup()
    _L0_gnn_in = {k: v for k, v in _L0_gnn_all.items() if k in ('W1', 'root1', 'b1', 'W2', 'root2', 'b2')}
    del _L0_gnn_all

    def _L0_mix_setup():
        import jax, jax.numpy as jnp
        import numpy as np
        import math
        B, N, C = (8, 512, 768)
        H = 12
        DH = C // H
        M = 256
        LN_EPS = 1e-05

        def _phi(t, random_features):
            norm_sq = 0.5 * jnp.sum(t * t, axis=-1, keepdims=True)
            proj = jnp.einsum('bhnd,md->bhnm', t, random_features)
            return jnp.exp(proj - norm_sq) * (1.0 / math.sqrt(M))
        key = jax.random.key(seed)
        ks = jax.random.split(key, 7)
        x = jax.random.normal(ks[0], (B, N, C), dtype=jnp.float32)
        W_qkv = jax.random.normal(ks[1], (C, 3 * C), dtype=jnp.float32) * (1.0 / math.sqrt(C))
        W_proj = jax.random.normal(ks[2], (C, C), dtype=jnp.float32) * (1.0 / math.sqrt(C))
        b_proj = jnp.zeros((C,), dtype=jnp.float32)
        gamma = jnp.ones((C,), dtype=jnp.float32)
        beta = jnp.zeros((C,), dtype=jnp.float32)
        random_features = jax.random.normal(ks[3], (M, DH), dtype=jnp.float32) / math.sqrt(DH)
        return {'x': x, 'W_qkv': W_qkv, 'W_proj': W_proj, 'b_proj': b_proj, 'gamma': gamma, 'beta': beta, 'random_features': random_features}
    _L0_mix_all = _L0_mix_setup()
    _L0_mix_in = {k: v for k, v in _L0_mix_all.items() if k in ('W_qkv', 'W_proj', 'b_proj', 'gamma', 'beta', 'random_features')}
    del _L0_mix_all

    def _L0_ffn_setup():
        import jax, jax.numpy as jnp
        import numpy as np
        DIM = 768
        NUM_HEADS = 12
        HEAD_DIM = DIM // NUM_HEADS
        SCALE = HEAD_DIM ** (-0.5)
        NUM_EXPERTS = 8
        RANK = 16
        ALPHA = 32
        TOPK = 2
        SCALING = ALPHA / RANK
        B, S = (8, 1024)
        key = jax.random.key(seed)
        ks = jax.random.split(key, 12)
        d, e, r = (DIM, NUM_EXPERTS, RANK)
        inp = {'x': jax.random.normal(ks[0], (B, S, d), jnp.float32), 'Wg': jax.random.normal(ks[1], (e, d), jnp.float32) * 0.02, 'bg': jax.random.normal(ks[2], (e,), jnp.float32) * 0.02, 'Wqkv': jax.random.normal(ks[3], (3 * d, d), jnp.float32) * 0.02, 'bqkv': jax.random.normal(ks[4], (3 * d,), jnp.float32) * 0.02, 'Wproj': jax.random.normal(ks[5], (d, d), jnp.float32) * 0.02, 'bproj': jax.random.normal(ks[6], (d,), jnp.float32) * 0.02, 'A': jax.random.normal(ks[7], (e, r, d), jnp.float32) * 0.05, 'ba': jax.random.normal(ks[8], (e, r), jnp.float32) * 0.02, 'Bm': jax.random.normal(ks[9], (e, 3 * d, r), jnp.float32) * 0.05, 'bb': jax.random.normal(ks[10], (e, 3 * d), jnp.float32) * 0.02}
        return inp
    _L0_ffn_all = _L0_ffn_setup()
    _L0_ffn_in = {k: v for k, v in _L0_ffn_all.items() if k in ('Wg', 'bg', 'Wqkv', 'bqkv', 'Wproj', 'bproj', 'A', 'ba', 'Bm', 'bb')}
    del _L0_ffn_all
    return {'x': x, 'src': src, 'dst': dst, 'edge_type_8': edge_type_8, 'L0_gnn_W1': _L0_gnn_in['W1'], 'L0_gnn_root1': _L0_gnn_in['root1'], 'L0_gnn_b1': _L0_gnn_in['b1'], 'L0_gnn_W2': _L0_gnn_in['W2'], 'L0_gnn_root2': _L0_gnn_in['root2'], 'L0_gnn_b2': _L0_gnn_in['b2'], 'L0_mix_W_qkv': _L0_mix_in['W_qkv'], 'L0_mix_W_proj': _L0_mix_in['W_proj'], 'L0_mix_b_proj': _L0_mix_in['b_proj'], 'L0_mix_gamma': _L0_mix_in['gamma'], 'L0_mix_beta': _L0_mix_in['beta'], 'L0_mix_random_features': _L0_mix_in['random_features'], 'L0_ffn_Wg': _L0_ffn_in['Wg'], 'L0_ffn_bg': _L0_ffn_in['bg'], 'L0_ffn_Wqkv': _L0_ffn_in['Wqkv'], 'L0_ffn_bqkv': _L0_ffn_in['bqkv'], 'L0_ffn_Wproj': _L0_ffn_in['Wproj'], 'L0_ffn_bproj': _L0_ffn_in['bproj'], 'L0_ffn_A': _L0_ffn_in['A'], 'L0_ffn_ba': _L0_ffn_in['ba'], 'L0_ffn_Bm': _L0_ffn_in['Bm'], 'L0_ffn_bb': _L0_ffn_in['bb']}

def reference(x, src, dst, edge_type_8, L0_gnn_W1, L0_gnn_root1, L0_gnn_b1, L0_gnn_W2, L0_gnn_root2, L0_gnn_b2, L0_mix_W_qkv, L0_mix_W_proj, L0_mix_b_proj, L0_mix_gamma, L0_mix_beta, L0_mix_random_features, L0_ffn_Wg, L0_ffn_bg, L0_ffn_Wqkv, L0_ffn_bqkv, L0_ffn_Wproj, L0_ffn_bproj, L0_ffn_A, L0_ffn_ba, L0_ffn_Bm, L0_ffn_bb):
    import jax
    import jax.numpy as jnp

    def _L0_gnn_ref(x, edge_index, edge_type, W1, root1, b1, W2, root2, b2):
        import jax, jax.numpy as jnp
        import numpy as np
        N, IN, OUT, R, E = (2500, 768, 768, 8, 40000)

        def _rgcn_conv(x, src, dst, etype, W, root, b):
            num_nodes = x.shape[0]
            num_rel = W.shape[0]
            x_src = x[src]
            seg = dst * num_rel + etype
            sums = jax.ops.segment_sum(x_src, seg, num_segments=num_nodes * num_rel)
            cnt = jax.ops.segment_sum(jnp.ones((src.shape[0],), dtype=x.dtype), seg, num_segments=num_nodes * num_rel)
            mean = sums / jnp.maximum(cnt, 1.0)[:, None]
            mean = mean.reshape(num_nodes, num_rel, -1)
            out = jnp.einsum('nri,rio->no', mean, W)
            return out + x @ root + b
        src, dst = (edge_index[0], edge_index[1])
        h = _rgcn_conv(x, src, dst, edge_type, W1, root1, b1)
        h = jax.nn.relu(h)
        out = _rgcn_conv(h, src, dst, edge_type, W2, root2, b2)
        return out

    def _L0_mix_ref(x, W_qkv, W_proj, b_proj, gamma, beta, random_features):
        import jax, jax.numpy as jnp
        import numpy as np
        import math
        B, N, C = (8, 512, 768)
        H = 12
        DH = C // H
        M = 256
        LN_EPS = 1e-05

        def _phi(t, random_features):
            norm_sq = 0.5 * jnp.sum(t * t, axis=-1, keepdims=True)
            proj = jnp.einsum('bhnd,md->bhnm', t, random_features)
            return jnp.exp(proj - norm_sq) * (1.0 / math.sqrt(M))
        b, n, c = x.shape
        qkv = (x @ W_qkv).reshape(b, n, 3, H, DH)
        qkv = jnp.transpose(qkv, (2, 0, 3, 1, 4))
        q, k, v = (qkv[0], qkv[1], qkv[2])
        q_p = _phi(q, random_features)
        k_p = _phi(k, random_features)
        kv = jnp.einsum('bhnm,bhnd->bhmd', k_p, v)
        out = jnp.einsum('bhnm,bhmd->bhnd', q_p, kv)
        k_sum = jnp.sum(k_p, axis=2)
        normalizer = jnp.einsum('bhnm,bhm->bhn', q_p, k_sum)[..., None]
        out = out / (normalizer + 1e-06)
        x_attn = jnp.transpose(out, (0, 2, 1, 3)).reshape(b, n, c)
        x_attn = x_attn @ W_proj + b_proj
        y = x + x_attn
        mu = jnp.mean(y, axis=-1, keepdims=True)
        var = jnp.mean(jnp.square(y - mu), axis=-1, keepdims=True)
        return (y - mu) * jax.lax.rsqrt(var + LN_EPS) * gamma + beta

    def _L0_ffn_ref(x, Wg, bg, Wqkv, bqkv, Wproj, bproj, A, ba, Bm, bb):
        import jax, jax.numpy as jnp
        import numpy as np
        DIM = 768
        NUM_HEADS = 12
        HEAD_DIM = DIM // NUM_HEADS
        SCALE = HEAD_DIM ** (-0.5)
        NUM_EXPERTS = 8
        RANK = 16
        ALPHA = 32
        TOPK = 2
        SCALING = ALPHA / RANK
        B, S = (8, 1024)
        b, s, d = x.shape
        t = b * s
        xf = x.reshape(t, d)
        probs = jax.nn.softmax(xf @ Wg.T + bg, axis=-1)
        top_w, top_idx = jax.lax.top_k(probs, TOPK)
        combine = jnp.zeros((t, NUM_EXPERTS), x.dtype).at[jnp.arange(t)[:, None], top_idx].add(top_w)
        h = jnp.einsum('td,erd->ter', xf, A) + ba
        hw = h * combine[:, :, None]
        delta = jnp.einsum('ter,eor->to', hw, Bm) + combine @ bb
        delta = delta * SCALING
        qkv = xf @ Wqkv.T + bqkv + delta
        qkv = qkv.reshape(b, s, 3, NUM_HEADS, HEAD_DIM)
        qkv = jnp.transpose(qkv, (2, 0, 3, 1, 4))
        q, k, v = (qkv[0], qkv[1], qkv[2])
        attn = jax.nn.softmax(jnp.einsum('bhsd,bhtd->bhst', q, k) * SCALE, axis=-1)
        out = jnp.einsum('bhst,bhtd->bhsd', attn, v)
        out = jnp.transpose(out, (0, 2, 1, 3)).reshape(b, s, d)
        return out @ Wproj.T + bproj
    edge_index = jnp.stack([src, dst])
    xn = _layernorm(x, axis=-1)
    x = x + _L0_gnn_ref(xn, edge_index, edge_type_8, L0_gnn_W1, L0_gnn_root1, L0_gnn_b1, L0_gnn_W2, L0_gnn_root2, L0_gnn_b2) + _L0_mix_ref(xn[None], L0_mix_W_qkv, L0_mix_W_proj, L0_mix_b_proj, L0_mix_gamma, L0_mix_beta, L0_mix_random_features)[0]
    x = x + _L0_ffn_ref(_layernorm(x, axis=-1)[None], L0_ffn_Wg, L0_ffn_bg, L0_ffn_Wqkv, L0_ffn_bqkv, L0_ffn_Wproj, L0_ffn_bproj, L0_ffn_A, L0_ffn_ba, L0_ffn_Bm, L0_ffn_bb)[0]
    return x

_drawn_inputs = setup_inputs


def setup_inputs(seed=0):
    import zlib

    import numpy as np

    out = dict(_drawn_inputs(seed))
    spreads = {'L0_gnn_b1': (0.0, 0.1),
     'L0_gnn_b2': (0.0, 0.283),
     'L0_mix_b_proj': (0.0, 0.28),
     'L0_mix_gamma': (1.0, 0.2),
     'L0_mix_beta': (0.0, 0.289)}
    factors = {'L0_mix_W_qkv': 8.0,
     'L0_mix_W_proj': 8.0,
     'L0_mix_random_features': 8.0,
     'L0_ffn_Wg': 7.495,
     'L0_ffn_bg': 8.0,
     'L0_ffn_bqkv': 8.0,
     'L0_ffn_bproj': 31.687,
     'L0_ffn_A': 4.851,
     'L0_ffn_ba': 8.0,
     'L0_ffn_Bm': 6.742,
     'L0_ffn_bb': 8.0}
    for name, (base, spread) in spreads.items():
        noise = np.random.default_rng([zlib.crc32(name.encode()), seed]).standard_normal(out[name].shape)
        drawn = base * np.exp(spread * noise) if base else spread * noise
        out[name] = jnp.asarray(drawn.astype(out[name].dtype))
    for name, factor in factors.items():
        out[name] = (out[name] * factor).astype(out[name].dtype)
    return out
```

```python
import concourse.bass as bass
from concourse import mybir
from concourse.alu_op_type import AluOpType as ALU
from contextlib import ExitStack

N, D, HEADS, DH, REL, EXPERTS = 1250, 768, 12, 64, 8, 8
E = 41250
ROWS = 125
RT = N // ROWS
KT = D // 128
HALF = D // 2
GRP = 4
GROUPS = -(-E // (GRP * 128))
TILES = GROUPS * GRP
PAD_DST = N
BATCH = TILES // (REL + 1)
PAIRS = HEADS // 2
MF = 256
LN_EPS = 1e-5
CHUNKS = ((0, 500), (500, 500), (1000, 250))
WM = KT * 3 * 128
W_GNN = 2 * (REL + 1)
W_MIX = W_GNN
W_LORA = W_MIX + PAIRS
LW = EXPERTS * 16
W_FFN = W_LORA + 1
KF = KT + 2
WF = KF * 3 * 128
W_OUT = W_FFN + PAIRS
X_SCALE = 256.0
TOP = 13
EXPONENT = 0x7F800000
TINY = 2.0 ** -60


def graph_and_attentions_kernel(nc, a, out):
    f32, f16, bf16, i32 = mybir.dt.float32, mybir.dt.float16, mybir.dt.bfloat16, mybir.dt.int32
    ACT = mybir.ActivationFunctionType
    AX = mybir.AxisListType
    top = ExitStack()
    with top:
        def sb(ctx, name, shape, dt):
            return ctx.enter_context(nc.sbuf_tensor(name, shape, dt))

        def sem(name):
            return top.enter_context(nc.semaphore(name))

        xn_rows = nc.dram_tensor("xn_rows", (N, D), f32).ap()
        gnn_rows = nc.dram_tensor("gnn_rows", (N, D), f32).ap()
        inv_table = nc.dram_tensor("inv_table", ((N + 1) * REL, 1), f32).ap()
        x2_rows = nc.dram_tensor("x2_rows", (N, D), f32).ap()
        msg_table = nc.dram_tensor("msg_table", (N * REL, D), f32).ap()
        msg_rows = msg_table.rearrange("(n r) c -> n r c", r=REL)

        XT = sb(top, "XT", [128, 2, KT, N], f16)
        hctx = ExitStack()
        HT = sb(hctx, "HT", [128, 2, KT, N], f16)
        hctx.close()
        HF = sb(top, "HF", [128, KT, N], f32)
        WST = sb(top, "WST", [128, KT * D], f32)
        wctx = ExitStack()
        WHL = sb(wctx, "WHL", [128, 2, 2, KT * D], f16)
        wctx.close()
        WHM = sb(top, "WHM", [128, 2, 2, WM], f16)
        pctx = ExitStack()
        WPR = sb(pctx, "WPR", [128, KT * D], f32)
        pctx.close()
        qctx = top.enter_context(ExitStack())
        F67 = sb(qctx, "F67", [128, 2 * 3 * 128], f32)
        QB = sb(qctx, "QB", [128, N], bf16)
        KB = sb(qctx, "KB", [128, N], bf16)
        FILL = sb(qctx, "FILL", [128, KT * D - 6 * 128 - N], f32)
        ROW = sb(top, "ROW", [ROWS, 4, D], f32)
        IDF = sb(top, "IDF", [128, 128], f32)
        STAT = sb(top, "STAT", [ROWS, 2, 24], f32)
        SC = sb(top, "SC", [128, 8], f32)
        SCI = SC[:].bitcast(i32)
        PMAX, PPOW, POW, WSCALE, WINV, XWINV = (slice(n_, n_ + 1) for n_ in range(6))
        ROWINV = sb(top, "ROWINV", [ROWS, RT], f32)
        OUTINV = sb(top, "OUTINV", [ROWS, RT], f32)
        HMX = sb(top, "HMX", [ROWS, 2, 4], f32)
        HMXI = HMX[:].bitcast(i32)
        gctx = ExitStack()
        ROOT = sb(gctx, "ROOT", [ROWS, RT, D], f32)
        MSG = sb(gctx, "MSG", [ROWS, 2, D], f32)
        GAT = sb(gctx, "GAT", [128, GRP, D], f32)
        HOT = sb(gctx, "HOT", [128, GRP, ROWS], f32)
        HOTC = sb(gctx, "HOTC", [128, GRP, ROWS], bf16)
        IDX4 = sb(gctx, "IDX4", [128, GRP], i32)
        IDXW = sb(gctx, "IDXW", [128, BATCH], i32)
        WGTW = sb(gctx, "WGTW", [128, BATCH], f32)
        BIAS = sb(gctx, "BIAS", [ROWS, D], f32)
        SRC = sb(gctx, "SRC", [128, TILES], i32)
        DST = sb(gctx, "DST", [128, TILES], i32)
        ETY = sb(gctx, "ETY", [128, TILES], i32)
        SKEY = sb(gctx, "SKEY", [128, TILES], i32)
        DKEY = sb(gctx, "DKEY", [128, TILES], i32)
        DSTF = sb(gctx, "DSTF", [128, TILES], f32)
        ETF = sb(gctx, "ETF", [128, TILES], f32)
        TMPF = sb(gctx, "TMPF", [128, TILES], f32)
        DLOC = sb(gctx, "DLOC", [128, TILES], f32)
        WALL = sb(gctx, "WALL", [128, TILES], f32)
        TYPEHOT = sb(gctx, "TYPEHOT", [128, TILES, REL], bf16)
        DSTG = sb(gctx, "DSTG", [GROUPS, GRP * 128], i32)
        IOTA = sb(gctx, "IOTA", [128, 128], bf16)
        CST = sb(gctx, "CST", [128, 160], f32)
        GB = sb(gctx, "GB", [GROUPS, 64], f32)
        LIMR = sb(gctx, "LIMR", [2 * RT, 4], f32)
        LIMF = sb(gctx, "LIMF", [1, 4 * RT], f32)
        LIM = sb(gctx, "LIM", [1, 2 * RT], i32)
        CNT = sb(gctx, "CNT", [128, 2, REL], f32)
        ZERO = sb(gctx, "ZERO", [128, HALF], bf16)
        ZF = sb(gctx, "ZF", [1, REL], f32)
        gctx.close()
        mctx = ExitStack()
        QA = sb(mctx, "QA", [128, 2, N], f32)
        KA = sb(mctx, "KA", [128, 2, N], f32)
        VA = sb(mctx, "VA", [ROWS, RT, 2, 128], f32)
        QP = sb(mctx, "QP", [128, 2, N], f32)
        KP = sb(mctx, "KP", [ROWS, RT, MF], f32)
        KV = sb(mctx, "KV", [128, 2, 128], f32)
        RF = sb(mctx, "RF", [128, 2, MF], f32)
        RCP = sb(mctx, "RCP", [64, 2, 500], f32)
        mctx.close()
        jctx = ExitStack()
        JR = sb(jctx, "JR", [ROWS, 2, 3, D], f32)
        VEC = sb(jctx, "VEC", [ROWS, 3, D], f32)
        jctx.close()
        fctx = ExitStack()
        LT = sb(fctx, "LT", [128, 2, N], f32)
        HG = sb(fctx, "HG", [ROWS, RT, 256], f32)
        BAG = sb(fctx, "BAG", [ROWS, LW + EXPERTS], f32)
        TRI = sb(fctx, "TRI", [128, EXPERTS * EXPERTS], f32)
        GP = sb(fctx, "GP", [ROWS, 3, RT, EXPERTS], f32)
        GM = sb(fctx, "GM", [ROWS, 2, RT], f32)
        GT = sb(fctx, "GT", [ROWS, 2, RT, EXPERTS * EXPERTS], f32)
        Q2 = sb(fctx, "Q2", [128, N], f32)
        K2 = sb(fctx, "K2", [128, N], f32)
        V2 = sb(fctx, "V2", [ROWS, 2, RT, 2, 128], bf16)
        NM = sb(fctx, "NM", [ROWS, 2, RT], f32)
        DG = sb(fctx, "DG", [ROWS, 2, N], bf16)
        PF = sb(fctx, "PF", [ROWS, 3, 500], f32)
        P2 = sb(fctx, "P2", [ROWS, 4, 2, 500], bf16)
        IDB = sb(fctx, "IDB", [128, 128], bf16)
        ONB = sb(fctx, "ONB", [128, 128], bf16)
        RCPF = sb(fctx, "RCPF", [64, 1, 500], f32)
        fctx.close()
        octx = ExitStack()
        OR = sb(octx, "OR", [ROWS, 2, D], f32)
        OB = sb(octx, "OB", [ROWS, D], f32)
        octx.close()
        PS = top.enter_context(nc.psum_tensor("PS", [128, 8, 512], f32))

        names = """consts_in x_in0 x_in1 x_free stat_done sd_done xn_done xn_stored xn_free xt_made t_hi t_free
            w_in w_max w_scaled w_hi w_lo wp_in acc_done pair_out msg_out msg_free bias_in bias_free
            edges_in zeros_made bounds_made bounds_t lim_row lim_t lim_made
            hot1_made hot1_used cnt_done inv_made inv_out inv_free inv_zero wgt_in wgt_done
            hot_made gat_in0 gat_in1 gat_in2 gat_in3 edge_used idx_made pe_tick pool_tick relu_made h_scale h_t h_hi h_free gnn_out row_free
            rf_in ones_made mix_pe mix_act mix_act_free mix_dve vec_in jr_in0 jr_in1 jr_free jr_made mp_done mp_free js_done js_sd
            lg_in lg_pe lg_free gate_in gate_ex gate_done lt_pe lt_free ffn_ready ffn_pe ffn_dve ffn_act ffn_hi ffn_lo av_done dg_made
            or_in0 or_in1 or_free or_made ob_in fp_done fp_free out_free out_out x2_out x2_free x2_made xf_made xf_t xf_hi xf_free""".split()
        S = {n: sem(n) for n in names}

        MIX = [(f"q{c}", "act") for c in range(3)] + [(f"k{c}", "act") for c in range(3)] + [(f"v{c}", "dve") for c in range(3)]
        for h in range(2):
            MIX += [(f"K{h}{u}", "act") for u in range(RT // 2)]
            MIX += [(f"Q{h}{m}{c}", "act") for m in range(2) for c in range(3)]
            MIX += [(f"kv{h}", "dve")] + [(f"o{h}{c}", "dve") for c in range(3)]

        FFN = [(f"q{c}", "dve", (c,)) for c in range(3)] + [(f"k{c}", "dve", (3 + c,)) for c in range(3)]
        FFN += [(f"v{c}", "dve", ((6, 7, 0)[c],)) for c in range(3)]
        FFN += [(f"M0{s_}", "dve", (0, 1, 2)) for s_ in range(RT)]
        SPLIT_AT = 44
        MAX_AT = 2
        LAG = 2
        for h in range(2):
            todo, rows = [(c, t) for c in range(3) for t in range(RT)], list(range(RT))

            def product(c, t):
                FFN.append((f"A{h}{c}{t}", "", ()))
                if t == RT - 1:
                    FFN.append((f"O{h}{c}", "dve", (6 + c % 2,)))

            for n_, (c, t) in enumerate(todo):
                FFN.append((f"S{h}{c}{t}", "act", (3 + n_ % 3,)))
                if h == 0 and n_ % 3 == 1:
                    FFN.append((f"M1{rows.pop(0)}", "dve", (0, 1, 2)))
                if n_ >= LAG:
                    product(*todo[n_ - LAG])
            for c, t in todo[-LAG:]:
                product(c, t)

        class Order:

            def __init__(self, results, name):
                kept = [r for r in results if r[1]]
                self.at = {r[0]: i for i, r in enumerate(kept)}
                self.by = [r[1] for r in kept]
                self.banks = [r[2] for r in kept]
                self.nth = [self.by[:i].count(e) + 1 for i, e in enumerate(self.by)]
                self.size = {e: self.by.count(e) for e in set(self.by)}
                self.name, self.n = name, len(kept)

            def bank(self, r):
                return self.banks[self.at[r]][0]

            def made(self, turn, r):
                return turn * self.n + (self.at[r] + 1)

            def taken(self, turn, r):
                i = self.at[r]
                return turn * self.size[self.by[i]] + (self.size[self.by[i]] + self.nth[i])

            def wait_banks(self, pe, turn, r):
                i, need = self.at[r], {}
                for b in self.banks[i]:
                    before = [k for k in range(i) if b in self.banks[k]]
                    k = before[-1] if before else max(k for k in range(self.n) if b in self.banks[k])
                    e = self.by[k]
                    need[e] = max(need.get(e, 0), self.nth[k] + (self.size[e] if before else 0))
                for e, v_ in sorted(need.items()):
                    pe.wait_ge(S[f"{self.name}_{e}"], turn * self.size[e] + v_)

        mix = Order([(r, e, (i % 8,)) for i, (r, e) in enumerate(MIX)], "mix")
        ffn = Order(FFN, "ffn")
        block = top.enter_context(nc.Block())

        def tview(b0):
            return PS[:, b0:b0 + 2, 0:3 * ROWS].rearrange("p b (k c) -> p b k c", c=ROWS)

        def xtview(T, part, t):
            return T[:, part, :, bass.ts(t, ROWS)].rearrange("p (b k) c -> p b k c", b=2)

        rowps = lambda b0: PS[0:ROWS, b0:b0 + 2, 0:HALF]
        halves = lambda ap: ap.rearrange("p (h c) -> p h c", h=2)

        @block.sync
        def _(sp):
            sp.dma_start(IDF[:], a["ident"]).then_inc(S["consts_in"], 16)
            with sp.Fori(0, RT // 2) as i:
                for j in range(2):
                    t = i * 2 + j
                    sp.wait_ge(S["x_free"], t + 1)
                    sp.dma_start(ROW[:, j, :], a["x"][bass.ts(t, ROWS), :]).then_inc(S[f"x_in{j}"], 16)
                for j in range(2):
                    t = i * 2 + j
                    sp.wait_ge(S["xn_done"], t + 1)
                    sp.dma_start(xn_rows[bass.ts(t, ROWS), :], ROW[:, 2 + j, :]).then_inc(S["xn_stored"], 16)
                    sp.wait_ge(S["xn_stored"], t * 16 + 16)
                    sp.sem_inc(S["xn_free"], 1)
            for dst, s in ((SRC, "srcT"), (DST, "dstT"), (ETY, "etT"), (DSTG, "dstG"), (CST, "cst")):
                sp.dma_start(dst[:], a[s]).then_inc(S["edges_in"], 16)
            sp.dma_start(WST[:], a["wg"][0:128, :]).then_inc(S["w_in"], 16)
            sp.wait_ge(S["zeros_made"], 1)
            sp.dma_start(inv_table[N * REL:(N + 1) * REL, :].rearrange("a b -> b a"), ZF[:]).then_inc(S["inv_zero"], 16)
            with sp.Fori(0, RT // 2) as i:
                for j in range(2):
                    b = i * 2 + j
                    sp.wait_ge(S["inv_made"], b + 3)
                    sp.dma_start(inv_table[bass.ts(b, ROWS * REL), :].rearrange("(p r) c -> p (r c)", r=REL),
                                 CNT[0:ROWS, j, :]).then_inc(S["inv_out"], 16)
                    sp.wait_ge(S["inv_out"], b * 16 + 16)
                    sp.sem_inc(S["inv_free"], 1)
            for L in range(2):
                sp.wait_ge(S["bias_free"], L + 1)
                sp.dma_start(BIAS[:], a["b1" if L == 0 else "b2"].broadcast_to([ROWS, D])).then_inc(S["bias_in"], 16)
                with sp.Fori(0, REL) as p:
                    sp.wait_ge(S["w_lo"], p + ((REL + 1) * L + 1))
                    sp.dma_start(WST[:], a["wg"][bass.ts(p + ((REL + 1) * L + 1), 128), :]).then_inc(S["w_in"], 16)
                    with sp.Fori(0, RT // 2) as i:
                        for j in range(2):
                            t = i * 2 + j
                            sp.wait_ge(S["pair_out"], p * RT + t + (100 * L + 3))
                            sp.dma_start(msg_rows[bass.ts(t, ROWS), bass.ds(p, 1), :].rearrange("n r c -> n (r c)"),
                                         MSG[:, j, :]).then_inc(S["msg_out"], 16)
                            sp.wait_ge(S["msg_out"], p * (16 * RT) + t * 16 + (L * 16 * REL * RT + 16))
                            sp.sem_inc(S["msg_free"], 1)
                if L == 0:
                    sp.wait_ge(S["w_lo"], REL + 1)
                    sp.dma_start(WST[:], a["wg"][bass.ts(REL + 1, 128), :]).then_inc(S["w_in"], 16)
            sp.wait_ge(S["w_lo"], W_MIX)
            sp.dma_start(WST[:, 0:WM], a["wm"][0:128, :]).then_inc(S["w_in"], 16)
            with sp.Fori(0, RT // 2) as i:
                for j in range(2):
                    b = i * 2 + j
                    sp.wait_ge(S["pair_out"], b + (190 + 3))
                    sp.dma_start(gnn_rows[bass.ts(b, ROWS), :], ROW[:, j, :]).then_inc(S["gnn_out"], 16)
                    sp.wait_ge(S["gnn_out"], b * 16 + 16)
                    sp.sem_inc(S["row_free"], 1)
            sp.dma_start(RF[:].rearrange("p a m -> p (a m)"), a["rf"]).then_inc(S["rf_in"], 16)
            sp.dma_start(WPR[:], a["wmp"]).then_inc(S["wp_in"], 16)
            with sp.Fori(0, PAIRS - 1) as it:
                sp.wait_ge(S["w_lo"], it + (W_MIX + 1))
                sp.dma_start(WST[:, 0:WM], a["wm"][bass.ts(it + 1, 128), :]).then_inc(S["w_in"], 16)
            sp.wait_ge(S["w_lo"], W_LORA)
            sp.dma_start(WST[:, 0:WM], a["wa"]).then_inc(S["w_in"], 16)
            sp.wait_ge(S["mix_dve"], mix.taken(PAIRS - 1, "o12"))
            for n_, key in enumerate(("bmp", "gamma", "beta")):
                sp.dma_start(VEC[:, n_, :], a[key].broadcast_to([ROWS, D])).then_inc(S["vec_in"], 16)
            with sp.Fori(0, RT // 2) as i:
                for j in range(2):
                    t = i * 2 + j
                    sp.wait_ge(S["jr_free"], t + 1)
                    for n_, rows in enumerate((xn_rows, a["x"], gnn_rows)):
                        sp.dma_start(JR[:, j, n_, :], rows[bass.ts(t, ROWS), :]).then_inc(S[f"jr_in{j}"], 16)
                for j in range(2):
                    t = i * 2 + j
                    sp.wait_ge(S["x2_made"], t + 1)
                    sp.dma_start(x2_rows[bass.ts(t, ROWS), :], ROW[:, j, :]).then_inc(S["x2_out"], 16)
                    sp.wait_ge(S["x2_out"], t * 16 + 16)
                    sp.sem_inc(S["x2_free"], 1)
            sp.dma_start(BAG[:], a["bag"].broadcast_to([ROWS, LW + EXPERTS])).then_inc(S["lg_in"], 16)
            sp.dma_start(TRI[:], a["tri"]).then_inc(S["lg_in"], 16)
            sp.wait_ge(S["w_lo"], W_LORA + 1)
            sp.dma_start(WST[:, 0:WF], a["wf"][0:128, :]).then_inc(S["w_in"], 16)
            with sp.Fori(0, PAIRS - 1) as it:
                sp.wait_ge(S["w_lo"], it + (W_FFN + 1))
                sp.dma_start(WST[:, 0:WF], a["wf"][bass.ts(it + 1, 128), :]).then_inc(S["w_in"], 16)
            sp.wait_ge(S["w_lo"], W_OUT)
            sp.dma_start(WST[:, 0:WF], a["wf"][(PAIRS - 1) * 128:PAIRS * 128, :]).then_inc(S["w_in"], 16)
            sp.wait_ge(S["w_lo"], W_OUT + 1)
            sp.dma_start(WST[:], a["wo"]).then_inc(S["wp_in"], 16)
            sp.wait_ge(S["ffn_dve"], ffn.taken(PAIRS - 1, "O12"))
            sp.dma_start(OB[:], a["bo"].broadcast_to([ROWS, D])).then_inc(S["ob_in"], 16)
            with sp.Fori(0, RT // 2) as i:
                for j in range(2):
                    t = i * 2 + j
                    sp.wait_ge(S["or_free"], t + 1)
                    sp.dma_start(OR[:, j, :], x2_rows[bass.ts(t, ROWS), :]).then_inc(S[f"or_in{j}"], 16)
                for j in range(2):
                    t = i * 2 + j
                    sp.wait_ge(S["fp_free"], t + 3)
                    sp.dma_start(out[bass.ts(t, ROWS), :], ROW[:, j, :]).then_inc(S["out_out"], 16)
                    sp.wait_ge(S["out_out"], t * 16 + 16)
                    sp.sem_inc(S["out_free"], 1)
            sp.wait_ge(S["out_out"], 16 * RT)

        @block.gpsimd
        def _(g):

            def scale(q, cols):
                g.wait_ge(S["w_max"], q + 1)
                g.sem_inc(S["pool_tick"], 1)
                g.partition_all_reduce(SC[:, POW], SC[:, PPOW], 128, bass.bass_isa.ReduceOp.max)
                g.drain()
                g.tensor_scalar(SC[:, POW], SC[:, POW], TINY, None, ALU.max)
                g.drain()
                g.tensor_scalar(SCI[:, WSCALE], SCI[:, POW], -1.0, float((254 + TOP) << 23), ALU.mult, ALU.add)
                g.tensor_scalar(SC[:, WINV], SC[:, POW], 2.0 ** -TOP, None, ALU.mult)
                g.tensor_scalar(SC[:, XWINV], SC[:, POW], 2.0 ** -TOP / X_SCALE, None, ALU.mult)
                g.drain()
                g.tensor_scalar(WST[:, 0:cols], WST[:, 0:cols], SC[:, WSCALE], None, ALU.mult).then_inc(S["w_scaled"], 1)

            def split_low(q, W=WHL, cols=KT * D, ranks=False):
                scale(q, WF if ranks else cols)
                g.wait_ge(S["w_hi"], q + 1)
                g.sem_inc(S["pool_tick"], 1)
                if ranks:
                    g.tensor_copy(F67[:], WST[:, WM:WF])
                    g.drain()
                g.tensor_tensor(W[:, bass.ds(q % 2, 1), 1, 0:cols].rearrange("p a c -> p (a c)"), WST[:, 0:cols],
                                W[:, bass.ds(q % 2, 1), 0, 0:cols].rearrange("p a c -> p (a c)"), ALU.subtract).then_inc(S["w_lo"], 1)

            def gather_weights(i):
                g.tensor_copy(IDXW[:], DKEY[:, bass.ts(i, BATCH)])
                g.drain()
                for j in range(BATCH):
                    g.indirect_dma_start(out=WGTW[:, j:j + 1], out_offset=None, in_=inv_table,
                                         in_offset=bass.IndirectOffsetOnAxis(ap=IDXW[:, j:j + 1], axis=0)).then_inc(S["wgt_in"], 16)
                g.wait_ge(S["wgt_in"], i * (16 * BATCH) + 16 * BATCH)
                g.tensor_copy(WALL[:, bass.ts(i, BATCH)], WGTW[:]).then_inc(S["wgt_done"], 1)
                g.drain()

            split_low(0)
            g.wait_ge(S["inv_out"], 16 * RT)
            g.wait_ge(S["inv_zero"], 16)
            with g.Fori(0, REL) as p:
                gather_weights(p)
                split_low(p + 1)
            gather_weights(REL)
            split_low(REL + 1)
            cnt = g.alloc_register("g_groups")
            g.reg_mov(cnt, 0)
            for L in range(2):
                if L == 1:
                    with g.Fori(0, REL) as p:
                        split_low(p + REL + 2)
                if L == 1:
                    split_low(W_MIX, WHM, WM)
                g.wait_ge(S["msg_out"], 16 * REL * RT * (L + 1))
                with g.Fori(0, RT) as b:
                    lo = g.value_load(LIM[0:1, bass.ts(b, 1)], min_val=0, max_val=GROUPS - 1)
                    hi = g.value_load(LIM[0:1, bass.ds(b + RT, 1)], min_val=1, max_val=GROUPS)
                    with g.Fori(lo, hi) as e:
                        n = g.snap(cnt, min_val=0, max_val=1 << 20)
                        for j in range(GRP):
                            g.wait_ge(S["idx_made"], n * GRP + (j + 1))
                            g.sem_inc(S["pool_tick"], 1)
                            g.indirect_dma_start(out=GAT[:, j, :], out_offset=None, in_=msg_table,
                                                 in_offset=bass.IndirectOffsetOnAxis(ap=IDX4[:, j:j + 1], axis=0)).then_inc(S[f"gat_in{j}"], 16)
                        g.reg_add(cnt, cnt, 1)
            with g.Fori(0, PAIRS - 1) as it:
                split_low(it + (W_MIX + 1), WHM, WM)
            split_low(W_LORA, WHM, WM)
            g.wait_ge(S["vec_in"], 3 * 16)
            with g.Fori(0, RT // 2) as i:
                for j in range(2):
                    g.wait_ge(S[f"jr_in{j}"], i * 48 + 48)
                    g.sem_inc(S["pool_tick"], 1)
                    g.tensor_tensor(JR[:, j, 0, :], JR[:, j, 0, :], VEC[:, 0, :], ALU.add)
                    g.tensor_tensor(JR[:, j, 1, :], JR[:, j, 1, :], JR[:, j, 2, :], ALU.add)
                    g.drain()
                    g.tensor_tensor(JR[:, j, 1, :], JR[:, j, 1, :], VEC[:, 2, :], ALU.add).then_inc(S["jr_made"], 1)
            g.wait_ge(S["mp_done"], RT)
            split_low(W_FFN, WHM, WM, ranks=True)
            with g.Fori(0, PAIRS) as it:
                for n_ in range(2 * 3 * RT):
                    h, c, t = n_ // 30, n_ // 10 % 3, n_ % 10
                    n = CHUNKS[c][1]
                    if n_ == SPLIT_AT:
                        split_low(it + (W_FFN + 1), WHM, WM, ranks=True)
                    g.wait_ge(S["ffn_act"], ffn.taken(it, f"S{h}{c}{t}"))
                    g.sem_inc(S["pool_tick"], 1)
                    g.tensor_tensor(P2[:, n_ % 4, 1, 0:n], PF[:, n_ % 3, 0:n], P2[:, n_ % 4, 0, 0:n], ALU.subtract).then_inc(S["ffn_lo"], 1)
            g.wait_ge(S["ob_in"], 16)
            with g.Fori(0, RT // 2) as i:
                for j in range(2):
                    g.wait_ge(S[f"or_in{j}"], i * 16 + 16)
                    g.sem_inc(S["pool_tick"], 1)
                    g.tensor_tensor(OR[:, j, :], OR[:, j, :], OB[:], ALU.add).then_inc(S["or_made"], 1)

        @block.scalar
        def _(act):
            with act.Fori(0, RT // 2) as i:
                for j in range(2):
                    t = i * 2 + j
                    act.wait_ge(S["stat_done"], t + 1)
                    act.activation(STAT[:, j, 15:16], STAT[:, j, 14:15], ACT.Sqrt).then_inc(S["sd_done"], 1)
                    act.wait_ge(S["xt_made"], t + 1)
                    act.activation(xtview(XT, 0, t), tview(2 * j), ACT.Copy, scale=X_SCALE).then_inc(S["t_hi"], 1)

            def split_high(q, done=None, W=WHL, cols=KT * D):
                if done is not None:
                    act.wait_ge(S["acc_done"], done)
                act.wait_ge(S["w_scaled"], q + 1)
                act.activation(W[:, bass.ds(q % 2, 1), 0, 0:cols].rearrange("p a c -> p (a c)"), WST[:, 0:cols], ACT.Copy).then_inc(S["w_hi"], 1)

            split_high(0, 1)
            for L in range(2):
                with act.Fori(0, REL) as p:
                    split_high(p + ((REL + 1) * L + 1), p * RT + (100 * L + 1))
                if L == 0:
                    split_high(REL + 1, REL * RT + 1)
                if L == 0:
                    with act.Fori(0, RT // 2) as i:
                        for j in range(2):
                            b = i * 2 + j
                            act.wait_ge(S["h_scale"], b + 1)
                            act.wait_ge(S["h_free"], b + 1)
                            act.activation(ROW[:, 2 + j, :], ROW[:, j, :], ACT.Relu, scale=HMX[:, j, 2:3]).then_inc(S["relu_made"], 1)
                        for j in range(2):
                            b = i * 2 + j
                            act.wait_ge(S["h_t"], b + 1)
                            act.activation(xtview(HT, 0, b), tview(4 + 2 * j), ACT.Copy).then_inc(S["h_hi"], 1)
            split_high(W_MIX, 100 + 80 + 1, WHM, WM)
            with act.Fori(0, PAIRS) as it:
                for T, x in ((QA, "q"), (KA, "k")):
                    for c, (c0, n) in enumerate(CHUNKS):
                        act.wait_ge(S["mix_pe"], mix.made(it, f"{x}{c}"))
                        p = PS[:, mix.bank(f"{x}{c}"), 0:n]
                        up, down = SC[0:64, XWINV], SC[64:128, XWINV]
                        act.activation(T[0:64, 0, c0:c0 + n], p[0:64, :], ACT.Copy, scale=up)
                        act.activation(T[64:128, 1, c0:c0 + n], p[64:128, :], ACT.Copy, scale=down)
                        act.activation(T[64:128, 0, c0:c0 + n], p[0:64, :], ACT.Square, scale=up)
                        act.activation(T[0:64, 1, c0:c0 + n], p[64:128, :], ACT.Square, scale=down).then_inc(S["mix_act"], 1)
                for h in range(2):
                    for u in range(RT // 2):
                        act.wait_ge(S["mix_pe"], mix.made(it, f"K{h}{u}"))
                        act.activation(KP[:, 2 * u:2 * u + 2, :].rearrange("p t m -> p (t m)"), PS[0:ROWS, mix.bank(f"K{h}{u}"), :], ACT.Exp).then_inc(S["mix_act"], 1)
                    for m in range(2):
                        for c, (c0, n) in enumerate(CHUNKS):
                            act.wait_ge(S["mix_pe"], mix.made(it, f"Q{h}{m}{c}"))
                            act.activation(QP[:, m, c0:c0 + n], PS[:, mix.bank(f"Q{h}{m}{c}"), 0:n], ACT.Exp).then_inc(S["mix_act"], 1)
                split_high(it + (W_MIX + 1), W=WHM, cols=WM)
            with act.Fori(0, RT // 2) as i:
                for j in range(2):
                    for k in range(2):
                        act.wait_ge(S["js_done"], i * 4 + (2 * j + k + 1))
                        act.activation(STAT[:, j, 15:16], STAT[:, j, 14:15], ACT.Sqrt).then_inc(S["js_sd"], 1)
                for j in range(2):
                    t = i * 2 + j
                    act.wait_ge(S["xf_t"], t + 1)
                    act.activation(xtview(XT, 0, t), tview(4 + 2 * j), ACT.Copy, scale=X_SCALE).then_inc(S["xf_hi"], 1)
            split_high(W_FFN, W=WHM, cols=WM)
            act.wait_ge(S["gate_in"], 1)
            act.activation(GP[:, 1], GP[:, 0], ACT.Exp).then_inc(S["gate_ex"], 1)
            for u in range(RT // 2):
                act.wait_ge(S["lt_pe"], u + 1)
                act.activation(LT[:, :, 2 * u * ROWS:2 * (u + 1) * ROWS], PS[:, 2 + u, 0:4 * ROWS].rearrange("p (k c) -> p k c", k=2), ACT.Copy,
                               scale=X_SCALE).then_inc(S["lt_free"], 1)
            with act.Fori(0, PAIRS) as it:
                for x, T in (("q", QB), ("k", KB)):
                    for c, (c0, n) in enumerate(CHUNKS):
                        act.wait_ge(S["ffn_pe"], ffn.made(it, f"{x}{c}"))
                        act.activation(T[:, c0:c0 + n], PS[:, ffn.bank(f"{x}{c}"), 0:n], ACT.Copy, scale=SC[:, XWINV]).then_inc(S["ffn_hi"], 1)
                for c in range(3):
                    t0, t1 = 4 * c, min(4 * c + 4, RT)
                    act.wait_ge(S["ffn_pe"], ffn.made(it, f"v{c}"))
                    act.activation(V2[:, 0, t0:t1, :, 0:64], PS[0:ROWS, ffn.bank(f"v{c}"), 0:(t1 - t0) * 128]
                                   .rearrange("p (t h d) -> p t h d", h=2, d=DH), ACT.Copy, scale=SC[0:ROWS, XWINV]).then_inc(S["ffn_hi"], 1)
                for n_ in range(2 * 3 * RT):
                    h, c, t = n_ // 30, n_ // 10 % 3, n_ % 10
                    n = CHUNKS[c][1]
                    p = PS[0:ROWS, ffn.bank(f"S{h}{c}{t}"), 0:n]
                    if n_ == SPLIT_AT:
                        split_high(it + (W_FFN + 1), W=WHM, cols=WM)
                    act.wait_ge(S["ffn_pe"], ffn.made(it, f"S{h}{c}{t}"))
                    act.wait_ge(S["ffn_lo"], it * 60 + (n_ + 1))
                    act.activation(PF[:, n_ % 3, 0:n], p, ACT.Exp, scale=DH ** -0.5)
                    act.wait_ge(S["av_done"], it * 60 + (n_ + 1))
                    act.activation(P2[:, n_ % 4, 0, 0:n], p, ACT.Exp, scale=DH ** -0.5).then_inc(S["ffn_act"], 1)

        @block.vector
        def _(v):
            v.memset(ZERO[:], 0.0).then_inc(S["zeros_made"], 1)
            v.memset(ZF[:], 0.0)
            v.drain()
            v.sem_inc(S["x_free"], 2)
            v.sem_inc(S["t_free"], 2)
            for n_, k_ in (("xn_free", 2), ("acc_done", 1), ("pair_out", 2), ("msg_free", 2), ("bias_free", 1), ("hot1_used", GRP),
                           ("edge_used", GRP), ("h_free", 2), ("row_free", 2), ("mix_act", mix.size["act"]), ("mix_dve", mix.size["dve"]), ("mp_free", 2), ("jr_free", 2),
                           ("x2_free", 2), ("lg_free", 2), ("ffn_dve", ffn.size["dve"]), ("ffn_act", ffn.size["act"]), ("ffn_lo", 3), ("av_done", 4),
                           ("or_free", 2), ("fp_free", 2), ("out_free", 2),  ("xf_free", 2), ("inv_free", 2), ("inv_made", 2)):
                v.sem_inc(S[n_], k_)

            def panel_max(q, cols=KT * D):
                v.wait_ge(S["w_in"], q * 16 + 16)
                v.tensor_reduce(SC[:, PMAX], WST[:, 0:cols], AX.X, ALU.max, apply_absolute_value=True)
                v.drain()
                v.tensor_scalar(SCI[:, PPOW], SCI[:, PMAX], EXPONENT, None, ALU.bitwise_and).then_inc(S["w_max"], 1)

            def inverse_sd(slot):
                var, sd, r, e = (STAT[:, slot, n_:n_ + 1] for n_ in (14, 15, 16, 17))
                v.reciprocal(r, sd)
                v.drain()
                v.tensor_scalar(e, r, r, var, ALU.mult, ALU.mult)
                v.drain()
                v.tensor_scalar(e, e, -0.5, 1.5, ALU.mult, ALU.add)
                v.drain()
                v.tensor_tensor(r, r, e, ALU.mult)
                v.drain()

            def statistics(slot, X):
                for h in range(2):
                    v.bn_stats(STAT[:, slot, 6 * h:6 * h + 6], X[:, h * HALF:(h + 1) * HALF])
                v.drain()
                v.bn_aggr(STAT[:, slot, 12:14], STAT[:, slot, 0:12])
                v.drain()
                v.tensor_scalar(STAT[:, slot, 14:15], STAT[:, slot, 13:14], LN_EPS, None, ALU.add).then_inc(S["stat_done"], 1)

            with v.Fori(0, RT // 2) as i:
                for j in range(2):
                    t = i * 2 + j
                    v.wait_ge(S[f"x_in{j}"], i * 16 + 16)
                    statistics(j, ROW[:, j, :])
                    v.wait_ge(S["sd_done"], t + 1)
                    inverse_sd(j)
                    v.wait_ge(S["t_free"], t + 1)
                    v.wait_ge(S["xn_free"], t + 1)
                    v.tensor_scalar(ROW[:, 2 + j, :], ROW[:, j, :], STAT[:, j, 12:13], STAT[:, j, 16:17],
                                    ALU.subtract, ALU.mult).then_inc(S["xn_done"], 1)
                    v.drain()
                    v.sem_inc(S["x_free"], 1)
                    v.wait_ge(S["t_hi"], t + 1)
                    v.scalar_tensor_tensor(xtview(XT, 1, t), tview(2 * j), X_SCALE, xtview(XT, 0, t), ALU.mult, ALU.subtract).then_inc(S["t_free"], 1)
            v.wait_ge(S["edges_in"], 5 * 16)
            v.tensor_copy(DSTF[:], DST[:])
            v.tensor_copy(ETF[:], ETY[:])
            v.tensor_copy(TMPF[:], SRC[:])
            v.tensor_copy(IOTA[:], CST[:, 0:128])
            v.drain()
            v.scalar_tensor_tensor(SKEY[:], TMPF[:], float(REL), ETF[:], ALU.mult, ALU.add)
            v.scalar_tensor_tensor(DKEY[:], DSTF[:], float(REL), ETF[:], ALU.mult, ALU.add)
            v.tensor_tensor(TYPEHOT[:], ETF[:].unsqueeze(2).broadcast_to([128, TILES, REL]),
                            IOTA[:, 0:REL].unsqueeze(1).broadcast_to([128, TILES, REL]), ALU.is_equal)
            v.tensor_reduce(GB[:, 0:1], DSTG[:], AX.X, ALU.min)
            v.tensor_reduce(GB[:, 1:2], DSTG[:], AX.X, ALU.max)
            v.drain()
            lbs, ubs, up, down = (CST[0:GROUPS, 128:138], CST[0:GROUPS, 138:148], CST[0:GROUPS, 148:149], CST[0:GROUPS, 149:150])
            v.tensor_scalar(GB[:, 4:14], lbs, GB[:, 1:2], None, ALU.is_le)
            v.tensor_scalar(GB[:, 14:24], ubs, GB[:, 0:1], None, ALU.is_gt)
            v.drain()
            v.tensor_tensor(GB[:, 24:34], GB[:, 4:14], GB[:, 14:24], ALU.mult)
            v.drain()
            v.tensor_scalar(GB[:, 40:50], GB[:, 24:34], down, None, ALU.mult)
            v.tensor_scalar(GB[:, 50:60], GB[:, 24:34], up, None, ALU.mult)
            v.drain()
            v.sem_inc(S["bounds_made"], 1)
            v.wait_ge(S["bounds_t"], 1)
            v.tensor_reduce(LIMR[:, 0:1], PS[0:2 * RT, 0, 0:GROUPS], AX.X, ALU.max).then_inc(S["lim_row"], 1)
            v.wait_ge(S["lim_t"], 1)
            v.tensor_scalar(LIMF[:, 0:RT], PS[0:1, 1, 0:RT], -1.0, float(GROUPS), ALU.mult, ALU.add)
            v.drain()
            v.tensor_scalar(LIMF[:, 2 * RT:3 * RT], LIMF[:, 0:RT], float(GROUPS - 1), None, ALU.min)
            v.drain()
            v.tensor_scalar(LIMF[:, 0:RT], LIMF[:, 2 * RT:3 * RT], 1.0, None, ALU.add)
            v.drain()
            v.tensor_tensor(LIMF[:, 3 * RT:4 * RT], LIMF[:, 0:RT], PS[0:1, 1, RT:2 * RT], ALU.max)
            v.drain()
            v.tensor_copy(LIM[:], LIMF[:, 2 * RT:4 * RT])
            v.drain()
            v.sem_inc(S["lim_made"], 1)

            panel_max(0)
            v.memset(ROWINV[:], 1.0 / X_SCALE)
            cnt = v.alloc_register("v_groups")
            v.reg_mov(cnt, 0)
            with v.Fori(0, RT // 2) as i:
                for j in range(2):
                    b = i * 2 + j
                    v.tensor_scalar(DLOC[:], DSTF[:], CST[:, bass.ds(b + 128, 1)], None, ALU.subtract)
                    v.drain()
                    lo = v.value_load(LIM[0:1, bass.ts(b, 1)], min_val=0, max_val=GROUPS - 1)
                    hi = v.value_load(LIM[0:1, bass.ds(b + RT, 1)], min_val=1, max_val=GROUPS)
                    with v.Fori(lo, hi) as e:
                        n = v.snap(cnt, min_val=0, max_val=1 << 20)
                        for k in range(GRP):
                            v.wait_ge(S["hot1_used"], n * GRP + (k + 1))
                            v.tensor_scalar(HOTC[:, k, :], IOTA[:, 0:ROWS], DLOC[:, bass.ds(e * GRP + k, 1)], None,
                                            ALU.is_equal).then_inc(S["hot1_made"], 1)
                        v.reg_add(cnt, cnt, 1)
                    v.wait_ge(S["cnt_done"], b + 1)
                    v.wait_ge(S["inv_free"], b + 1)
                    v.tensor_scalar(CNT[0:ROWS, j, :], PS[0:ROWS, 2 + j, 0:REL], 1.0, None, ALU.max)
                    v.drain()
                    v.reciprocal(CNT[0:ROWS, j, :], CNT[0:ROWS, j, :])
                    v.drain()
                    v.sem_inc(S["inv_made"], 1)

            v.reg_mov(cnt, 0)
            for L in range(2):
                def out_scales(q):
                    v.drain()
                    v.wait_ge(S["w_lo"], q + 1)
                    v.tensor_scalar(OUTINV[:], ROWINV[:], SC[0:ROWS, WINV], None, ALU.mult)
                    v.drain()

                with v.Fori(0, REL) as p:
                    q = p + (REL + 1) * L
                    out_scales(q)
                    for part in ((0, MAX_AT), (MAX_AT, RT // 2)):
                        with v.Fori(*part) as i:
                            for j in range(2):
                                t = i * 2 + j
                                v.wait_ge(S["acc_done"], p * RT + t + (100 * L + 2))
                                v.wait_ge(S["msg_free"], p * RT + t + (REL * RT * L + 1))
                                v.tensor_scalar(halves(MSG[:, j, :]), rowps(2 * j), OUTINV[:, bass.ts(t, 1)], None, ALU.mult).then_inc(S["pair_out"], 1)
                        if part[0] == 0:
                            panel_max(q + 1)
                v.wait_ge(S["bias_in"], 16 * (L + 1))
                out_scales((REL + 1) * L + REL)
                for part in ((0, MAX_AT), (MAX_AT, RT // 2)):
                    with v.Fori(*part) as i:
                        for j in range(2):
                            t = i * 2 + j
                            v.wait_ge(S["acc_done"], t + (100 * L + 80 + 2))
                            v.scalar_tensor_tensor(halves(ROOT[:, bass.ts(t, 1), :].rearrange("p a c -> p (a c)")), rowps(2 * j), OUTINV[:, bass.ts(t, 1)],
                                                   halves(BIAS[:]), ALU.mult, ALU.add).then_inc(S["pair_out"], 1)
                    if part[0] == 0:
                        panel_max((REL + 1) * (L + 1), KT * D if L == 0 else WM)
                v.drain()
                v.sem_inc(S["bias_free"], 1)
                if L == 0:
                    v.wait_ge(S["wgt_done"], REL + 1)
                with v.Fori(0, RT // 2) as i:
                    for j in range(2):
                        b = i * 2 + j
                        v.tensor_scalar(DLOC[:], DSTF[:], CST[:, bass.ds(b + 128, 1)], None, ALU.subtract)
                        v.drain()
                        lo = v.value_load(LIM[0:1, bass.ts(b, 1)], min_val=0, max_val=GROUPS - 1)
                        hi = v.value_load(LIM[0:1, bass.ds(b + RT, 1)], min_val=1, max_val=GROUPS)
                        with v.Fori(lo, hi) as e:
                            n = v.snap(cnt, min_val=0, max_val=1 << 20)
                            for k in range(GRP):
                                v.wait_ge(S["edge_used"], n * GRP + (k + 1))
                                v.tensor_copy(IDX4[:, k:k + 1], SKEY[:, bass.ds(e * GRP + k, 1)]).then_inc(S["idx_made"], 1)
                                v.tensor_scalar(HOT[:, k, :], IOTA[:, 0:ROWS], DLOC[:, bass.ds(e * GRP + k, 1)],
                                                WALL[:, bass.ds(e * GRP + k, 1)], ALU.is_equal, ALU.mult).then_inc(S["hot_made"], 1)
                            v.reg_add(cnt, cnt, 1)
                        v.wait_ge(S["acc_done"], b + (100 * L + 90 + 2))
                        if L == 1:
                            v.wait_ge(S["row_free"], b + 1)
                        v.tensor_tensor(halves(ROW[:, j, :]), rowps(2 * j),
                                        halves(ROOT[:, bass.ts(b, 1), :].rearrange("p a c -> p (a c)")), ALU.add).then_inc(S["pair_out"], 1)
                        if L == 0:
                            v.drain()
                            v.tensor_reduce(HMX[:, j, 0:1], ROW[:, j, :], AX.X, ALU.max)
                            v.drain()
                            v.tensor_scalar(HMX[:, j, 0:1], HMX[:, j, 0:1], TINY, None, ALU.max)
                            v.drain()
                            v.tensor_scalar(HMXI[:, j, 1:2], HMXI[:, j, 0:1], EXPONENT, None, ALU.bitwise_and)
                            v.drain()
                            v.tensor_scalar(HMXI[:, j, 2:3], HMXI[:, j, 1:2], -1.0, float((254 + TOP) << 23), ALU.mult, ALU.add)
                            v.tensor_scalar(ROWINV[:, bass.ts(b, 1)], HMX[:, j, 1:2], 2.0 ** -TOP, None, ALU.mult)
                            v.drain()
                            v.sem_inc(S["h_scale"], 1)
                    if L == 0:
                        for j in range(2):
                            b = i * 2 + j
                            v.wait_ge(S["h_hi"], b + 1)
                            v.tensor_tensor(xtview(HT, 1, b), tview(4 + 2 * j), xtview(HT, 0, b), ALU.subtract).then_inc(S["h_free"], 1)
            v.drain()
            v.memset(VA[:, :, :, 64:128], 1.0).then_inc(S["ones_made"], 1)

            def normalise(psum, n, c0, it, h, eps, RC):
                r, o = RC[:, 0, 0:n], HF[64 * h:64 * h + 64, bass.ds(it, 1), c0:c0 + n].rearrange("p a c -> p (a c)")
                if eps:
                    v.tensor_scalar(r, psum[64:128, 0:n], eps, None, ALU.add)
                    v.drain()
                    v.reciprocal(r, r)
                else:
                    v.reciprocal(r, psum[64:128, 0:n])
                v.drain()
                return v.tensor_tensor(o, psum[0:64, 0:n], r, ALU.mult)

            with v.Fori(0, PAIRS) as it:
                for c in range(3):
                    t0, t1 = 4 * c, min(4 * c + 4, RT)
                    v.wait_ge(S["mix_pe"], mix.made(it, f"v{c}"))
                    v.tensor_scalar(VA[:, t0:t1, :, 0:64], PS[0:ROWS, mix.bank(f"v{c}"), 0:(t1 - t0) * 128]
                                    .rearrange("p (t h d) -> p t h d", h=2, d=DH), SC[0:ROWS, XWINV], None, ALU.mult).then_inc(S["mix_dve"], 1)
                for h in range(2):
                    v.wait_ge(S["mix_pe"], mix.made(it, f"kv{h}"))
                    v.tensor_scalar(KV[:].rearrange("p m d -> p (m d)"), PS[:, mix.bank(f"kv{h}"), 0:256], 1.0 / MF, None, ALU.mult).then_inc(S["mix_dve"], 1)
                    if h == 0:
                        panel_max(it + (W_MIX + 1), WM)
                    for c, (c0, n) in enumerate(CHUNKS):
                        v.wait_ge(S["mix_pe"], mix.made(it, f"o{h}{c}"))
                        normalise(PS[:, mix.bank(f"o{h}{c}"), :], n, c0, it, h, 1e-6, RCP).then_inc(S["mix_dve"], 1)
                        v.drain()

            with v.Fori(0, RT // 2) as i:
                for j in range(2):
                    t = i * 2 + j
                    Y = ROW[:, j, :]

                    def scaled(out, k):
                        for h in range(2):
                            v.bn_stats(STAT[:, j, 6 * h:6 * h + 6], Y[:, h * HALF:(h + 1) * HALF])
                        v.drain()
                        v.bn_aggr(STAT[:, j, 12:14], STAT[:, j, 0:12])
                        v.drain()
                        v.tensor_scalar(STAT[:, j, 14:15], STAT[:, j, 13:14], LN_EPS, None, ALU.add).then_inc(S["js_done"], 1)
                        v.wait_ge(S["js_sd"], i * 4 + (2 * j + k + 1))
                        inverse_sd(j)
                        return v.tensor_scalar(out, Y, STAT[:, j, 12:13], STAT[:, j, 16:17], ALU.subtract, ALU.mult)

                    v.wait_ge(S["mp_done"], t + 1)
                    v.wait_ge(S["jr_made"], t + 1)
                    v.wait_ge(S["x2_free"], t + 1)
                    v.tensor_tensor(halves(Y), rowps(2 * j), halves(JR[:, j, 0, :]), ALU.add).then_inc(S["mp_free"], 1)
                    v.drain()
                    scaled(Y, 0)
                    v.drain()
                    v.tensor_tensor(Y, Y, VEC[:, 1, :], ALU.mult)
                    v.drain()
                    v.tensor_tensor(Y, Y, JR[:, j, 1, :], ALU.add).then_inc(S["x2_made"], 1)
                    v.drain()
                    v.sem_inc(S["jr_free"], 1)
                    v.wait_ge(S["xf_free"], t + 1)
                    scaled(ROW[:, 2 + j, :], 1).then_inc(S["xf_made"], 1)
                for j in range(2):
                    t = i * 2 + j
                    v.wait_ge(S["xf_hi"], t + 1)
                    v.scalar_tensor_tensor(xtview(XT, 1, t), tview(4 + 2 * j), X_SCALE, xtview(XT, 0, t), ALU.mult, ALU.subtract).then_inc(S["xf_free"], 1)
            v.drain()
            v.memset(HG[:], 0.0)
            v.drain()
            v.memset(HG[:, :, LW + EXPERTS:LW + EXPERTS + 1], 1.0)
            v.tensor_copy(IDB[:], IDF[:])
            v.memset(ONB[:], 1.0)
            v.memset(V2[:, 0, :, :, 64:128], 1.0)
            v.memset(V2[:, 1, :, :, 64:128], 0.0)
            v.drain()
            v.sem_inc(S["ffn_ready"], 1)
            v.wait_ge(S["lg_in"], 32)
            with v.Fori(0, RT // 2) as i:
                for j in range(2):
                    t = i * 2 + j
                    v.wait_ge(S["lg_pe"], t + 1)
                    v.scalar_tensor_tensor(HG[:, bass.ts(t, 1), 0:LW + EXPERTS].rearrange("p a c -> p (a c)"), PS[0:ROWS, j, 0:LW + EXPERTS],
                                           SC[0:ROWS, XWINV], BAG[:], ALU.mult, ALU.add).then_inc(S["lg_free"], 1)
            v.drain()
            panel_max(W_FFN, WF)
            over = lambda ap: ap.unsqueeze(2).broadcast_to([ROWS, RT, EXPERTS])
            LOG = HG[:, :, LW:LW + EXPERTS]
            v.tensor_reduce(GM[:, 0, :], LOG, AX.X, ALU.max)
            v.drain()
            v.tensor_tensor(GP[:, 0], LOG, over(GM[:, 0, :]), ALU.subtract).then_inc(S["gate_in"], 1)
            v.wait_ge(S["gate_ex"], 1)
            v.tensor_reduce(GM[:, 0, :], GP[:, 1], AX.X, ALU.add)
            v.drain()
            v.reciprocal(GM[:, 1, :], GM[:, 0, :])
            v.drain()
            v.tensor_tensor(GP[:, 0], GP[:, 1], over(GM[:, 1, :]), ALU.mult)
            v.drain()
            sq = [ROWS, RT, EXPERTS, EXPERTS]
            mine, others = GP[:, 0].unsqueeze(3).broadcast_to(sq), GP[:, 0].unsqueeze(2).broadcast_to(sq)
            g4 = lambda k: GT[:, k].rearrange("p t (e f) -> p t e f", f=EXPERTS)
            v.tensor_tensor(g4(0), others, mine, ALU.is_gt)
            v.tensor_tensor(g4(1), others, mine, ALU.is_equal)
            v.drain()
            v.tensor_tensor(GT[:, 1], GT[:, 1], TRI[0:ROWS].unsqueeze(1).broadcast_to([ROWS, RT, EXPERTS * EXPERTS]), ALU.mult)
            v.drain()
            v.tensor_tensor(GT[:, 0], GT[:, 0], GT[:, 1], ALU.add)
            v.drain()
            v.tensor_reduce(GP[:, 1], g4(0), AX.X, ALU.add)
            v.drain()
            v.tensor_scalar(GP[:, 2], GP[:, 1], 2.0, 2.0, ALU.is_lt, ALU.mult)
            v.drain()
            v.tensor_tensor(LOG, GP[:, 2], GP[:, 0], ALU.mult)
            v.drain()
            v.tensor_tensor(HG[:, :, 0:LW].rearrange("p t (e r) -> p t e r", r=16), HG[:, :, 0:LW].rearrange("p t (e r) -> p t e r", r=16),
                            LOG.unsqueeze(3).broadcast_to([ROWS, RT, EXPERTS, 16]), ALU.mult).then_inc(S["gate_done"], 1)
            with v.Fori(0, PAIRS) as it:
                for n_, (x, T) in enumerate((("q", Q2), ("k", K2))):
                    for c, (c0, n) in enumerate(CHUNKS):
                        v.wait_ge(S["ffn_hi"], it * 9 + (3 * n_ + c + 1))
                        v.tensor_scalar(T[:, c0:c0 + n], PS[:, ffn.bank(f"{x}{c}"), 0:n], SC[:, XWINV], None, ALU.mult).then_inc(S["ffn_dve"], 1)
                for c in range(3):
                    t0, t1 = 4 * c, min(4 * c + 4, RT)
                    v.wait_ge(S["ffn_hi"], it * 9 + (6 + c + 1))
                    for t in range(t0, t1):
                        ins = v.scalar_tensor_tensor(V2[:, 1, t, :, 0:64], PS[0:ROWS, ffn.bank(f"v{c}"), (t - t0) * 128:(t - t0 + 1) * 128]
                                                     .rearrange("p (h d) -> p h d", d=DH), SC[0:ROWS, XWINV], V2[:, 0, t, :, 0:64], ALU.mult, ALU.subtract)
                    ins.then_inc(S["ffn_dve"], 1)
                for r in (r for r, e, _ in FFN if e == "dve" and r[0] in "MO"):
                    v.wait_ge(S["ffn_pe"], ffn.made(it, r))
                    h = int(r[1])
                    if r[0] == "M":
                        s_ = int(r[2])
                        v.tensor_reduce(NM[:, h, s_:s_ + 1], PS[0:ROWS, 0:3, :].rearrange("p b c -> p (b c)")[:, 0:N], AX.X, ALU.max,
                                        negate=True).then_inc(S["ffn_dve"], 1)
                        v.drain()
                        v.tensor_scalar(DG[:, h, s_ * ROWS:(s_ + 1) * ROWS], IDB[0:ROWS, 0:ROWS], NM[:, h, s_:s_ + 1], None, ALU.mult).then_inc(S["dg_made"], 1)
                        if r == "M19":
                            panel_max(it + (W_FFN + 1), WF)
                    else:
                        c0, n = CHUNKS[int(r[2])]
                        normalise(PS[:, ffn.bank(r), :], n, c0, it, h, 0, RCPF).then_inc(S["ffn_dve"], 1)
                        v.drain()
            with v.Fori(0, RT // 2) as i:
                for j in range(2):
                    t = i * 2 + j
                    v.wait_ge(S["fp_done"], t + 1)
                    v.wait_ge(S["or_made"], t + 1)
                    v.wait_ge(S["out_free"], t + 1)
                    v.tensor_tensor(halves(ROW[:, j, :]), rowps(2 * j), halves(OR[:, j, :]), ALU.add).then_inc(S["fp_free"], 1)
                    v.drain()
                    v.sem_inc(S["or_free"], 1)

        @block.tensor
        def _(pe):
            def six_transposes(b0, slot, S_done):
                for k in range(KT):
                    o = PS[:, b0 + k // 3, (k % 3) * ROWS:(k % 3 + 1) * ROWS]
                    ins = pe.transpose(o, ROW[:, slot, k * 128:(k + 1) * 128], IDF[0:ROWS, 0:ROWS])
                ins.then_inc(S_done, 1)

            pe.wait_ge(S["consts_in"], 16)
            with pe.Fori(0, RT // 2) as i:
                for j in range(2):
                    t = i * 2 + j
                    pe.wait_ge(S["xn_done"], t + 1)
                    pe.wait_ge(S["t_free"], t + 1)
                    six_transposes(2 * j, 2 + j, S["xt_made"])
            pe.wait_ge(S["t_free"], RT + 2)
            pe.wait_ge(S["bounds_made"], 1)
            pe.transpose(PS[0:2 * RT, 0, 0:GROUPS], GB[:, 40:60], IDF[0:GROUPS, 0:GROUPS]).then_inc(S["bounds_t"], 1)
            pe.wait_ge(S["lim_row"], 1)
            pe.transpose(PS[0:1, 1, 0:2 * RT], LIMR[:, 0:1], IDF[0:2 * RT, 0:2 * RT]).then_inc(S["lim_t"], 1)
            pe.wait_ge(S["lim_made"], 1)
            cnt = pe.alloc_register("p_groups")
            pe.reg_mov(cnt, 0)
            with pe.Fori(0, RT // 2) as i:
                for j in range(2):
                    b = i * 2 + j
                    lo = pe.value_load(LIM[0:1, bass.ts(b, 1)], min_val=0, max_val=GROUPS - 1)
                    hi = pe.value_load(LIM[0:1, bass.ds(b + RT, 1)], min_val=1, max_val=GROUPS)
                    pe.wait_ge(S["inv_made"], b + 1)
                    pe.matmul(PS[0:ROWS, 2 + j, 0:REL], ZERO[:, 0:ROWS], ZERO[:, 0:REL], start=True, stop=False)
                    with pe.Fori(lo, hi) as e:
                        n = pe.snap(cnt, min_val=0, max_val=1 << 20)
                        for k in range(GRP):
                            pe.wait_ge(S["hot1_made"], n * GRP + (k + 1))
                            pe.matmul(PS[0:ROWS, 2 + j, 0:REL], HOTC[:, k, :], TYPEHOT[:, bass.ds(e * GRP + k, 1), :].rearrange("p a r -> p (a r)"),
                                      start=False, stop=False).then_inc(S["hot1_used"], 1)
                        pe.reg_add(cnt, cnt, 1)
                    pe.matmul(PS[0:ROWS, 2 + j, 0:REL], ZERO[:, 0:ROWS], ZERO[:, 0:REL], start=False, stop=True).then_inc(S["cnt_done"], 1)

            def row_products(X, t, slot, b0, done):
                for k in range(KT):
                    for xp, wps in ((0, (0, 1)), (1, (0,))):
                        for wp in wps:
                            for h in range(2):
                                ins = pe.matmul(PS[0:ROWS, b0 + h, 0:HALF], X[:, xp, k, bass.ts(t, ROWS)],
                                                WHL[:, bass.ds(slot, 1), wp, k * D + h * HALF:k * D + (h + 1) * HALF].rearrange("p a c -> p (a c)"),
                                                start=k == 0 and xp + wp == 0, stop=k == KT - 1 and xp == 1)
                ins.then_inc(done, 1)

            def full_products(t, W, b0, done):
                for k in range(KT):
                    for h in range(2):
                        ins = pe.matmul(PS[0:ROWS, b0 + h, 0:HALF], HF[:, k, t * ROWS:(t + 1) * ROWS],
                                        W[:, k * D + h * HALF:k * D + (h + 1) * HALF], start=k == 0, stop=k == KT - 1)
                ins.then_inc(done, 1)

            pe.reg_mov(cnt, 0)
            pe.wait_ge(S["inv_made"], RT + 2)
            for L in range(2):
                X = XT if L == 0 else HT
                if L == 1:
                    pe.wait_ge(S["h_free"], RT + 2)
                with pe.Fori(0, REL + 1) as p:
                    pe.wait_ge(S["w_lo"], p + ((REL + 1) * L + 1))
                    pe.sem_inc(S["pe_tick"], 1)
                    slot = (p + L) % 2
                    with pe.Fori(0, RT // 2) as i:
                        for j in range(2):
                            t = i * 2 + j
                            pe.wait_ge(S["pair_out"], p * RT + t + (100 * L + 1))
                            row_products(X, t, slot, 2 * j, S["acc_done"])
                with pe.Fori(0, RT // 2) as i:
                    for j in range(2):
                        b = i * 2 + j
                        lo = pe.value_load(LIM[0:1, bass.ts(b, 1)], min_val=0, max_val=GROUPS - 1)
                        hi = pe.value_load(LIM[0:1, bass.ds(b + RT, 1)], min_val=1, max_val=GROUPS)
                        pe.wait_ge(S["pair_out"], b + (100 * L + 90 + 1))
                        for h in range(2):
                            pe.matmul(PS[0:ROWS, 2 * j + h, 0:HALF], ZERO[:, 0:ROWS], ZERO[:], start=True, stop=False)
                        with pe.Fori(lo, hi) as e:
                            n = pe.snap(cnt, min_val=0, max_val=1 << 20)
                            for k in range(GRP):
                                pe.wait_ge(S["hot_made"], n * GRP + (k + 1))
                                pe.wait_ge(S[f"gat_in{k}"], n * 16 + 16)
                                for h in range(2):
                                    ins = pe.matmul(PS[0:ROWS, 2 * j + h, 0:HALF], HOT[:, k, :], GAT[:, k, h * HALF:(h + 1) * HALF],
                                                    start=False, stop=False)
                                ins.then_inc(S["edge_used"], 1)
                            pe.reg_add(cnt, cnt, 1)
                        for h in range(2):
                            ins = pe.matmul(PS[0:ROWS, 2 * j + h, 0:HALF], ZERO[:, 0:ROWS], ZERO[:], start=False, stop=True)
                        ins.then_inc(S["acc_done"], 1)
                    if L == 0:
                        for j in range(2):
                            b = i * 2 + j
                            pe.wait_ge(S["relu_made"], b + 1)
                            pe.wait_ge(S["h_free"], b + 1)
                            six_transposes(4 + 2 * j, 2 + j, S["h_t"])
            pe.wait_ge(S["pair_out"], 200 + 2)
            pe.wait_ge(S["ones_made"], 1)
            pe.wait_ge(S["rf_in"], 16)
            with pe.Fori(0, PAIRS) as it:
                slot = it % 2
                pe.wait_ge(S["w_lo"], it + (W_MIX + 1))
                pe.sem_inc(S["pe_tick"], 1)

                def w(part, k, x):
                    return WHM[:, bass.ds(slot, 1), part, (k * 3 + x) * 128:(k * 3 + x + 1) * 128].rearrange("p a c -> p (a c)")

                for x, nm in ((0, "q"), (1, "k")):
                    for c, (c0, n) in enumerate(CHUNKS):
                        mix.wait_banks(pe, it, f"{nm}{c}")
                        for k in range(KT):
                            for wp, xp in ((0, 0), (0, 1), (1, 0)):
                                ins = pe.matmul(PS[:, mix.bank(f"{nm}{c}"), 0:n], w(wp, k, x), XT[:, xp, k, c0:c0 + n],
                                                start=k == 0 and wp + xp == 0, stop=k == KT - 1 and wp == 1)
                        ins.then_inc(S["mix_pe"], 1)
                for c in range(3):
                    mix.wait_banks(pe, it, f"v{c}")
                    for t in range(4 * c, min(4 * c + 4, RT)):
                        for k in range(KT):
                            for xp, wp in ((0, 0), (0, 1), (1, 0)):
                                ins = pe.matmul(PS[0:ROWS, mix.bank(f"v{c}"), (t % 4) * 128:(t % 4) * 128 + 128],
                                                XT[:, xp, k, t * ROWS:(t + 1) * ROWS], w(wp, k, 2),
                                                start=k == 0 and wp + xp == 0, stop=k == KT - 1 and xp == 1)
                    ins.then_inc(S["mix_pe"], 1)
                for h in range(2):
                    if h == 0:
                        pe.wait_ge(S["mix_act"], mix.taken(it, "k2"))
                    for u in range(RT // 2):
                        mix.wait_banks(pe, it, f"K{h}{u}")
                        for t in (2 * u, 2 * u + 1):
                            ins = pe.matmul(PS[0:ROWS, mix.bank(f"K{h}{u}"), (t % 2) * MF:(t % 2 + 1) * MF],
                                            KA[:, h, t * ROWS:(t + 1) * ROWS], RF[:, h, :], start=True, stop=True)
                        ins.then_inc(S["mix_pe"], 1)
                    for m in range(2):
                        for c, (c0, n) in enumerate(CHUNKS):
                            mix.wait_banks(pe, it, f"Q{h}{m}{c}")
                            pe.matmul(PS[:, mix.bank(f"Q{h}{m}{c}"), 0:n], RF[:, h, m * 128:(m + 1) * 128], QA[:, h, c0:c0 + n],
                                      start=True, stop=True).then_inc(S["mix_pe"], 1)
                    mix.wait_banks(pe, it, f"kv{h}")
                    pe.wait_ge(S["mix_act"], mix.taken(it, f"K{h}4"))
                    pe.wait_ge(S["mix_dve"], mix.taken(it, "v2"))
                    for m in range(2):
                        for t in range(RT):
                            ins = pe.matmul(PS[:, mix.bank(f"kv{h}"), m * 128:(m + 1) * 128], KP[:, t, m * 128:(m + 1) * 128],
                                            VA[:, t, h, :], start=t == 0, stop=t == RT - 1)
                    ins.then_inc(S["mix_pe"], 1)
                    pe.wait_ge(S["mix_dve"], mix.taken(it, f"kv{h}"))
                    pe.wait_ge(S["mix_act"], mix.taken(it, f"Q{h}12"))
                    for c, (c0, n) in enumerate(CHUNKS):
                        mix.wait_banks(pe, it, f"o{h}{c}")
                        for m in range(2):
                            ins = pe.matmul(PS[:, mix.bank(f"o{h}{c}"), 0:n], KV[:, m, :], QP[:, m, c0:c0 + n], start=m == 0, stop=m == 1)
                        ins.then_inc(S["mix_pe"], 1)
            pe.wait_ge(S["mix_dve"], mix.taken(PAIRS - 1, "o12"))
            pe.wait_ge(S["wp_in"], 16)
            for i in range(RT // 2):
                for j in range(2):
                    t = i * 2 + j
                    pe.wait_ge(S["mp_free"], t + 1)
                    full_products(t, WPR, 2 * j, S["mp_done"])
                for j in range(2):
                    t = i * 2 + j
                    pe.wait_ge(S["xf_made"], t + 1)
                    pe.wait_ge(S["xf_free"], t + 1)
                    six_transposes(4 + 2 * j, 2 + j, S["xf_t"])
            pe.wait_ge(S["w_lo"], W_LORA + 1)
            pe.wait_ge(S["xf_free"], RT + 2)
            pe.wait_ge(S["mp_free"], RT + 2)
            with pe.Fori(0, RT // 2) as i:
                for j in range(2):
                    t = i * 2 + j
                    pe.wait_ge(S["lg_free"], t + 1)
                    for k in range(KT):
                        for xp, wp in ((0, 0), (0, 1), (1, 0)):
                            ins = pe.matmul(PS[0:ROWS, j, 0:LW + EXPERTS], XT[:, xp, k, bass.ts(t, ROWS)],
                                            WHM[:, W_LORA % 2, wp, k * (LW + EXPERTS):(k + 1) * (LW + EXPERTS)],
                                            start=k == 0 and xp + wp == 0, stop=k == KT - 1 and xp == 1)
                    ins.then_inc(S["lg_pe"], 1)
            pe.wait_ge(S["gate_done"], 1)
            for u in range(RT // 2):
                for k in range(2):
                    for t in range(2):
                        ins = pe.transpose(PS[:, 2 + u, (2 * k + t) * ROWS:(2 * k + t + 1) * ROWS],
                                           HG[:, 2 * u + t, k * 128:(k + 1) * 128], IDF[0:ROWS, 0:ROWS])
                ins.then_inc(S["lt_pe"], 1)
            pe.wait_ge(S["lt_free"], RT // 2)
            pe.wait_ge(S["ffn_ready"], 1)
            with pe.Fori(0, PAIRS) as it:
                pe.wait_ge(S["w_lo"], it + (W_FFN + 1))
                pe.sem_inc(S["pe_tick"], 1)
                slot = (it + W_FFN) % 2

                def wf(part, k, x):
                    return WHM[:, bass.ds(slot, 1), part, (k * 3 + x) * 128:(k * 3 + x + 1) * 128].rearrange("p a c -> p (a c)")

                def ranks(k, x):
                    return F67[:, (k * 3 + x) * 128:(k * 3 + x + 1) * 128]

                for x, nm in ((0, "q"), (1, "k")):
                    for c, (c0, n) in enumerate(CHUNKS):
                        ffn.wait_banks(pe, it, f"{nm}{c}")
                        for k in range(KT):
                            for wp, xp in ((0, 0), (0, 1), (1, 0)):
                                pe.matmul(PS[:, ffn.bank(f"{nm}{c}"), 0:n], wf(wp, k, x), XT[:, xp, k, c0:c0 + n],
                                          start=k == 0 and wp + xp == 0, stop=False)
                        for k in range(2):
                            ins = pe.matmul(PS[:, ffn.bank(f"{nm}{c}"), 0:n], ranks(k, x), LT[:, k, c0:c0 + n], start=False, stop=k == 1)
                        ins.then_inc(S["ffn_pe"], 1)
                for c in range(3):
                    ffn.wait_banks(pe, it, f"v{c}")
                    for t in range(4 * c, min(4 * c + 4, RT)):
                        o = PS[0:ROWS, ffn.bank(f"v{c}"), (t % 4) * 128:(t % 4) * 128 + 128]
                        for k in range(KT):
                            for xp, wp in ((0, 0), (0, 1), (1, 0)):
                                pe.matmul(o, XT[:, xp, k, t * ROWS:(t + 1) * ROWS], wf(wp, k, 2), start=k == 0 and wp + xp == 0, stop=False)
                        for k in range(2):
                            ins = pe.matmul(o, LT[:, k, t * ROWS:(t + 1) * ROWS], ranks(k, 2), start=False, stop=k == 1)
                    ins.then_inc(S["ffn_pe"], 1)
                for r, e, _ in FFN:
                    if r[0] in "qkvO":
                        continue
                    h = int(r[1])
                    half = slice(64 * h, 64 * h + 64)
                    if r[0] == "M":
                        s_ = int(r[2])
                        if r == "M00":
                            pe.wait_ge(S["ffn_dve"], ffn.taken(it, "k2"))
                        ffn.wait_banks(pe, it, r)
                        for b in range(3):
                            n = min(512, N - 512 * b)
                            ins = pe.matmul(PS[0:ROWS, b, 0:n], QB[half, s_ * ROWS:(s_ + 1) * ROWS], KB[half, 512 * b:512 * b + n],
                                            start=True, stop=True)
                        ins.then_inc(S["ffn_pe"], 1)
                    elif r[0] == "S":
                        c, t = int(r[2]), int(r[3])
                        c0, n = CHUNKS[c]
                        if t == 0:
                            pe.wait_ge(S["dg_made"], it * (2 * RT) + (h * RT + min(4 * c + 4, RT)))
                        ffn.wait_banks(pe, it, r)
                        p = PS[0:ROWS, ffn.bank(r), 0:n]
                        pe.matmul(p, K2[half, t * ROWS:(t + 1) * ROWS], Q2[half, c0:c0 + n], start=True, stop=False)
                        pe.matmul(p, ONB[0:ROWS, 0:ROWS], DG[:, h, c0:c0 + n], start=False, stop=True).then_inc(S["ffn_pe"], 1)
                    else:
                        c, t = int(r[2]), int(r[3])
                        n, k = CHUNKS[c][1], h * 30 + c * 10 + t
                        if t == 0:
                            ffn.wait_banks(pe, it, f"O{h}{c}")
                            if h == 0 and c == 0:
                                pe.wait_ge(S["ffn_dve"], ffn.taken(it, "v2"))
                        pe.wait_ge(S["ffn_lo"], it * 60 + (k + 4))
                        o = PS[:, ffn.bank(f"O{h}{c}"), 0:n]
                        for vp, pp in ((0, 0), (0, 1), (1, 0)):
                            ins = pe.matmul(o, V2[:, vp, t, h, :], P2[:, k % 4, pp, 0:n], start=t == 0 and vp + pp == 0, stop=t == RT - 1 and vp == 1)
                        if t == RT - 1:
                            ins.then_inc(S["ffn_pe"], 1)
                            pe.drain().then_inc(S["av_done"], 1)
                        else:
                            ins.then_inc(S["av_done"], 1)
            pe.wait_ge(S["wp_in"], 32)
            pe.wait_ge(S["ffn_dve"], ffn.taken(PAIRS - 1, "O12"))
            for i in range(RT // 2):
                for j in range(2):
                    pe.wait_ge(S["fp_free"], i * 2 + (j + 1))
                    full_products(i * 2 + j, WST, 2 * j, S["fp_done"])


def lay_out(np, inp):
    a = {k: np.asarray(v) for k, v in inp.items()}
    pad = TILES * 128 - E

    def edges(v, fill):
        return np.concatenate([v, np.full(pad, fill, v.dtype)])

    def slices(w):
        return w.reshape(-1, 128, w.shape[1]).transpose(1, 0, 2)

    o = {"x": a["x"], "ident": np.eye(128, dtype=np.float32)}
    for name, key, fill in (("srcT", "src", 0), ("dstT", "dst", PAD_DST), ("etT", "edge_type_8", 0)):
        o[name] = np.ascontiguousarray(edges(a[key], fill).reshape(TILES, 128).T)
    o["dstG"] = edges(a["dst"], PAD_DST).reshape(GROUPS, GRP * 128)
    cst = np.zeros((128, 160), np.float32)
    cst[:, 0:128] = np.arange(128)
    cst[:, 128:138] = ROWS * np.arange(RT)
    cst[:, 138:148] = ROWS * (np.arange(RT) + 1)
    cst[:, 148] = np.arange(128) + 1
    cst[:, 149] = GROUPS - np.arange(128)
    o["cst"] = cst
    o["wg"] = np.concatenate([slices(w).reshape(128, KT * D) for l in "12"
                              for w in [*a[f"L0_gnn_W{l}"], a[f"L0_gnn_root{l}"]]])
    o["b1"], o["b2"] = a["L0_gnn_b1"].reshape(1, D), a["L0_gnn_b2"].reshape(1, D)
    wqkv = a["L0_mix_W_qkv"].reshape(KT, 128, 3, PAIRS, 128)
    o["wm"] = np.ascontiguousarray(wqkv.transpose(3, 1, 0, 2, 4)).reshape(PAIRS * 128, WM)
    rft, half = a["L0_mix_random_features"].T, np.full((DH, MF), -0.5, np.float32)
    o["rf"] = np.concatenate([np.concatenate([rft, half]), np.concatenate([half, rft])], axis=1)
    o["wmp"] = slices(a["L0_mix_W_proj"]).reshape(128, KT * D)
    o["bmp"], o["gamma"], o["beta"] = (a[f"L0_mix_{n}"].reshape(1, D) for n in ("b_proj", "gamma", "beta"))
    wa = slices(np.concatenate([a["L0_ffn_A"].reshape(LW, D), a["L0_ffn_Wg"]]).T).reshape(128, -1)
    o["wa"] = np.concatenate([wa, np.zeros((128, WM - wa.shape[1]), np.float32)], axis=1)
    o["bag"] = np.concatenate([a["L0_ffn_ba"].reshape(LW), a["L0_ffn_bg"]])[None]
    o["tri"] = np.tile(np.tril(np.ones((EXPERTS, EXPERTS), np.float32), -1).reshape(1, -1), (128, 1))
    wf = np.concatenate([a["L0_ffn_Wqkv"].T, a["L0_ffn_Bm"].transpose(0, 2, 1).reshape(LW, 3 * D), a["L0_ffn_bb"],
                         a["L0_ffn_bqkv"][None], np.zeros((128 - EXPERTS - 1, 3 * D), np.float32)])
    o["wf"] = np.ascontiguousarray(wf.reshape(KF, 128, 3, PAIRS, 128).transpose(3, 1, 0, 2, 4)).reshape(PAIRS * 128, WF)
    o["wo"] = slices(a["L0_ffn_Wproj"].T).reshape(128, KT * D)
    o["bo"] = a["L0_ffn_bproj"].reshape(1, D)
    return {k: np.ascontiguousarray(v) for k, v in o.items()}


def kernel(**inputs):
    import numpy as _np
    import concourse.bacc as _bacc
    from concourse import mybir as _mybir
    from concourse.bass_utils import run_bass_kernel_spmd as _run

    nc = _bacc.Bacc("TRN2", target_bir_lowering=False, num_devices=1)
    arrays, a = {}, {}
    for name, v in lay_out(_np, inputs).items():
        arrays[f"in_{name}_dram"] = v
        a[name] = nc.dram_tensor(f"in_{name}_dram", v.shape, _mybir.dt.from_np(v.dtype), kind="ExternalInput").ap()
    out = nc.dram_tensor("out_0_dram", (N, D), _mybir.dt.float32, kind="ExternalOutput").ap()
    graph_and_attentions_kernel(nc, a, out)
    r = _run(nc, [arrays], core_ids=[0])
    return r.results[0]["out_0_dram"]
```

```python
import concourse.bass as bass
from concourse import mybir
from concourse.alu_op_type import AluOpType as ALU
from contextlib import ExitStack

N, D, HEADS, DH, REL, EXPERTS = 1250, 768, 12, 64, 8, 8
E = 41250
ROWS = 125
RT = N // ROWS
KT = D // 128
HALF = D // 2
GRP = 5
GROUPS = -(-E // (GRP * 128))
TILES = GROUPS * GRP
PAD_DST = N
BATCH = -(-TILES // REL)
RING = 12
PAIRS = HEADS // 2
MF = 256
LN_EPS = 1e-5
CHUNKS = ((0, 500), (500, 500), (1000, 250))
WM = KT * 3 * 128
W_GNN = 2 * (REL + 1)
W_MIX = W_GNN
W_LORA = W_MIX + PAIRS
LW = EXPERTS * 16
W_FFN = W_LORA + 1
KF = KT + 2
WF = KF * 3 * 128
W_OUT = W_FFN + PAIRS
X_SCALE = 256.0
TOP = 13
EXPONENT = 0x7F800000
TINY = 2.0 ** -60


def graph_and_attentions_kernel(nc, a, out):
    f32, f16, bf16, i32 = mybir.dt.float32, mybir.dt.float16, mybir.dt.bfloat16, mybir.dt.int32
    ACT = mybir.ActivationFunctionType
    AX = mybir.AxisListType
    top = ExitStack()
    with top:
        def sb(ctx, name, shape, dt):
            return ctx.enter_context(nc.sbuf_tensor(name, shape, dt))

        def sem(name):
            return top.enter_context(nc.semaphore(name))

        xn_rows = nc.dram_tensor("xn_rows", (N, D), f32).ap()
        gnn_rows = nc.dram_tensor("gnn_rows", (N, D), f32).ap()
        inv_table = nc.dram_tensor("inv_table", ((N + 1) * REL, 1), f32).ap()
        x2_rows = nc.dram_tensor("x2_rows", (N, D), f32).ap()
        msg_table = nc.dram_tensor("msg_table", (N * REL, D), f32).ap()
        msg_rows = msg_table.rearrange("(n r) c -> n r c", r=REL)

        XT = sb(top, "XT", [128, 2, KT, N], f16)
        hctx = ExitStack()
        HT = sb(hctx, "HT", [128, 2, KT, N], f16)
        hctx.close()
        HF = sb(top, "HF", [128, KT, N], f32)
        WST = sb(top, "WST", [128, KT * D], f32)
        wctx = ExitStack()
        WHL = sb(wctx, "WHL", [128, 2, 2, KT * D], f16)
        wctx.close()
        WHM = sb(top, "WHM", [128, 2, 2, WM], f16)
        pctx = ExitStack()
        WPR = sb(pctx, "WPR", [128, KT * D], f32)
        pctx.close()
        qctx = top.enter_context(ExitStack())
        F67 = sb(qctx, "F67", [128, 2 * 3 * 128], f32)
        QS = sb(qctx, "QS", [128, 2, N], f16)
        QL = sb(qctx, "QL", [128, N], f16)
        FILL = sb(qctx, "FILL", [128, KT * D - 6 * 128 - 3 * N // 2], f32)
        ROW = sb(top, "ROW", [ROWS, 4, D], f32)
        IDF = sb(top, "IDF", [128, 128], f32)
        LNS = sb(top, "LNS", [ROWS, RT, 14], f32)
        LNR = sb(top, "LNR", [ROWS, 4, RT], f32)
        STAT = sb(top, "STAT", [ROWS, 2, 24], f32)
        SC = sb(top, "SC", [128, 8], f32)
        SCI = SC[:].bitcast(i32)
        PMAX, PPOW, POW, WSCALE, WINV, XWINV = (slice(n_, n_ + 1) for n_ in range(6))
        ROWINV = sb(top, "ROWINV", [ROWS, RT], f32)
        OUTINV = sb(top, "OUTINV", [ROWS, RT], f32)
        HMX = sb(top, "HMX", [ROWS, 2, 4], f32)
        HMXI = HMX[:].bitcast(i32)
        gctx = ExitStack()
        ROOT = sb(gctx, "ROOT", [ROWS, RT, D], f32)
        MSG = sb(gctx, "MSG", [ROWS, 2, D], f32)
        cctx = ExitStack()
        HOTC = sb(cctx, "HOTC", [128, RING * GRP, ROWS], bf16)
        cctx.close()
        GAT = sb(gctx, "GAT", [128, GRP, D], f32)
        HOT = sb(gctx, "HOT", [128, GRP, ROWS], f32)
        IDXG = sb(gctx, "IDXG", [128, GRP], i32)
        IDXW = sb(gctx, "IDXW", [128, BATCH], i32)
        WGTW = sb(gctx, "WGTW", [128, BATCH], f32)
        BIAS = sb(gctx, "BIAS", [ROWS, D], f32)
        SRC = sb(gctx, "SRC", [128, TILES], i32)
        DST = sb(gctx, "DST", [128, TILES], i32)
        ETY = sb(gctx, "ETY", [128, TILES], i32)
        SKEY = sb(gctx, "SKEY", [128, TILES], i32)
        DKEY = sb(gctx, "DKEY", [128, BATCH * REL], i32)
        DSTF = sb(gctx, "DSTF", [128, TILES], f32)
        ETF = sb(gctx, "ETF", [128, TILES], f32)
        TMPF = sb(gctx, "TMPF", [128, TILES], f32)
        DLOC = sb(gctx, "DLOC", [128, TILES], f32)
        WALL = sb(gctx, "WALL", [128, BATCH * REL], f32)
        TYPEHOT = sb(gctx, "TYPEHOT", [128, TILES, REL], bf16)
        DSTG = sb(gctx, "DSTG", [GROUPS, GRP * 128], i32)
        IOTA = sb(gctx, "IOTA", [128, 128], bf16)
        CST = sb(gctx, "CST", [128, 160], f32)
        GB = sb(gctx, "GB", [GROUPS, 64], f32)
        LIMR = sb(gctx, "LIMR", [2 * RT, 4], f32)
        LIMF = sb(gctx, "LIMF", [1, 4 * RT], f32)
        LIM = sb(gctx, "LIM", [1, 2 * RT], i32)
        CNT = sb(gctx, "CNT", [128, 2, REL], f32)
        ZERO = sb(gctx, "ZERO", [128, HALF], bf16)
        ZF = sb(gctx, "ZF", [1, REL], f32)
        gctx.close()
        mctx = ExitStack()
        QA = sb(mctx, "QA", [128, 2, N], f32)
        KA = sb(mctx, "KA", [128, 2, N], f32)
        VA = sb(mctx, "VA", [ROWS, RT, 2, 128], f32)
        QP = sb(mctx, "QP", [128, 2, N], f32)
        KP = sb(mctx, "KP", [ROWS, RT, MF], f32)
        KV = sb(mctx, "KV", [128, 2, 128], f32)
        RF = sb(mctx, "RF", [128, 2, MF], f32)
        RCP = sb(mctx, "RCP", [128, N], f32)
        NUM = sb(mctx, "NUM", [128, N], f32)
        mctx.close()
        jctx = ExitStack()
        JR = sb(jctx, "JR", [ROWS, 2, 3, D], f32)
        JP = sb(jctx, "JP", [ROWS, 4, 2, D], f32)
        VEC = sb(jctx, "VEC", [ROWS, 3, D], f32)
        jctx.close()
        fctx = ExitStack()
        LT = sb(fctx, "LT", [128, 2, N], f32)
        HG = sb(fctx, "HG", [ROWS, RT, 256], f32)
        BAG = sb(fctx, "BAG", [ROWS, LW + EXPERTS], f32)
        TRI = sb(fctx, "TRI", [128, EXPERTS * EXPERTS], f32)
        GP = sb(fctx, "GP", [ROWS, 3, RT, EXPERTS], f32)
        GM = sb(fctx, "GM", [ROWS, 2, RT], f32)
        GT = sb(fctx, "GT", [ROWS, 2, RT, EXPERTS * EXPERTS], f32)
        KS = sb(fctx, "KS", [128, 2, N], f16)
        QK = sb(fctx, "QK", [128, 8], f32)
        QKI = QK[:].bitcast(i32)
        LMAX, LPOW, LALL, QKS, QKINV, SINV, SSCALE = (slice(n_, n_ + 1) for n_ in range(7))
        V2 = sb(fctx, "V2", [ROWS, 2, RT, 2, 128], bf16)
        NM = sb(fctx, "NM", [ROWS, 2, RT], f32)
        DG = sb(fctx, "DG", [ROWS, 2, N], bf16)
        PF = sb(fctx, "PF", [ROWS, 4, 500], f32)
        P2 = sb(fctx, "P2", [ROWS, 6, 2, 500], bf16)
        IDB = sb(fctx, "IDB", [128, 128], bf16)
        ONB = sb(fctx, "ONB", [128, 128], bf16)
        RCPF = sb(fctx, "RCPF", [64, 1, 500], f32)
        fctx.close()
        octx = ExitStack()
        OR = sb(octx, "OR", [ROWS, 2, D], f32)
        OB = sb(octx, "OB", [ROWS, D], f32)
        octx.close()
        PS = top.enter_context(nc.psum_tensor("PS", [128, 8, 512], f32))

        names = """consts_in x_in0 x_in1 stat_done sd_done xn_done xn_stored xn_free xt_made t_hi t_free
            w_in w_max w_scale w_hi w_lo wp_in acc_done pair_out msg_out msg_free bias_in bias_free
            edges_in zeros_made bounds_made bounds_t lim_row lim_t lim_made
            hot1_made hot1_used cnt_done inv_made inv_out inv_free inv_zero wgt_in wgt_done
            hot_made gat_in0 gat_in1 gat_in2 gat_in3 gat_in4 gat_in5 edge_used idx_made pe_tick pool_tick relu_made h_scale h_t h_hi h_free gnn_out row_free
            rf_in ones_made mix_pe mix_act mix_dve vec_in jr_in0 jr_in1 hf_made jr_free jp_free jr_made mp_done mp_free js_done js_sd
            lg_in lg_pe lg_free gate_in gate_ex gate_done qk_scale s_scale lt_max lt_pow lt_pe lt_free ffn_ready ffn_pe ffn_dve ffn_act ffn_hi ffn_lo av_done dg0_made dg1_made
            or_in0 or_in1 or_free or_made ob_in fp_done fp_free out_free out_out x2_out x2_free x2_made xf_made xf_t xf_hi xf_free""".split()
        S = {n: sem(n) for n in names}

        MIX = [(f"q{c}", "act") for c in range(3)] + [(f"k{c}", "act") for c in range(3)] + [(f"v{c}", "dve") for c in range(3)]
        for h in range(2):
            MIX += [(f"K{h}{u}", "act") for u in range(RT // 2)]
            if h == 1:
                MIX += [(f"o0{c}", "dve") for c in range(3)]
            MIX += [(f"Q{h}{m}{c}", "act") for m in range(2) for c in range(3)]
            MIX += [(f"kv{h}", "dve")]
        MIX += [(f"o1{c}", "dve") for c in range(3)]

        FFN = [(f"q{c}", "dve", (c,)) for c in range(3)] + [(f"k{c}", "dve", (3 + c,)) for c in range(3)]
        for t in range(RT):
            FFN.append((f"W{t}", "", ()))
            if t % 4 == 3 or t == RT - 1:
                FFN.append((f"v{t // 4}", "dve", ((6, 7, 6)[t // 4],)))
            FFN.append((f"M0{t}", "dve", ((3, 4, 5), (0, 1, 2))[t % 2]))
        SPLIT_AT = 38
        PARTS = ((0, 2), (2, 4), (4, 5))
        LAG = (2, 4)
        EXPS, PARTED = 4, 6
        waiting, rows = [], list(range(RT))

        def product():
            h, c, t = waiting.pop(0)
            FFN.append((f"A{h}{c}{t}", "", ()))
            if t == RT - 1:
                FFN.append((f"O{h}{c}", "dve", (6 + (3 * h + c) % 2,)))

        for n_ in range(2 * 3 * RT):
            h, c, t = n_ // 30, n_ // 10 % 3, n_ % 10
            FFN.append((f"S{h}{c}{t}", "act", (3 + n_ % 3 if h == 0 else n_ % 6,)))
            if h == 0 and n_ % 3 == 1:
                FFN.append((f"M1{rows.pop(0)}", "dve", (0, 1, 2)))
            waiting.append((h, c, t))
            while len(waiting) > LAG[h]:
                product()
        while waiting:
            product()

        class Order:

            def __init__(self, results, name):
                kept = [r for r in results if r[1]]
                self.at = {r[0]: i for i, r in enumerate(kept)}
                self.by = [r[1] for r in kept]
                self.banks = [r[2] for r in kept]
                self.nth = [self.by[:i].count(e) + 1 for i, e in enumerate(self.by)]
                self.size = {e: self.by.count(e) for e in set(self.by)}
                self.name, self.n = name, len(kept)

            def bank(self, r):
                return self.banks[self.at[r]][0]

            def made(self, turn, r):
                return turn * self.n + (self.at[r] + 1)

            def taken(self, turn, r):
                i = self.at[r]
                return turn * self.size[self.by[i]] + (self.size[self.by[i]] + self.nth[i])

            def wait_banks(self, pe, turn, r):
                i, need = self.at[r], {}
                for b in self.banks[i]:
                    before = [k for k in range(i) if b in self.banks[k]]
                    k = before[-1] if before else max(k for k in range(self.n) if b in self.banks[k])
                    e = self.by[k]
                    need[e] = max(need.get(e, 0), self.nth[k] + (self.size[e] if before else 0))
                for e, v_ in sorted(need.items()):
                    pe.wait_ge(S[f"{self.name}_{e}"], turn * self.size[e] + v_)

        mix = Order([(r, e, (i % 8,)) for i, (r, e) in enumerate(MIX)], "mix")
        ffn = Order(FFN, "ffn")
        block = top.enter_context(nc.Block())

        def tview(b0):
            return PS[:, b0:b0 + 2, 0:3 * ROWS].rearrange("p b (k c) -> p b k c", c=ROWS)

        def block_bounds(eng, b):
            return (eng.value_load(LIM[0:1, bass.ts(b, 1)], min_val=0, max_val=GROUPS - 1),
                    eng.value_load(LIM[0:1, bass.ds(b + RT, 1)], min_val=1, max_val=GROUPS))

        def xtview(T, part, t):
            return T[:, part, :, bass.ts(t, ROWS)].rearrange("p (b k) c -> p b k c", b=2)

        rowps = lambda b0: PS[0:ROWS, b0:b0 + 2, 0:HALF]
        halves = lambda ap: ap.rearrange("p (h c) -> p h c", h=2)

        @block.sync
        def _(sp):
            sp.dma_start(IDF[:], a["ident"]).then_inc(S["consts_in"], 16)
            for h in range(2):
                sp.dma_start(ROOT[:, h * RT // 2:(h + 1) * RT // 2, :],
                             a["x"][h * N // 2:(h + 1) * N // 2, :].rearrange("(t p) c -> p t c", p=ROWS)).then_inc(S[f"x_in{h}"], 16)
            sp.dma_start(WST[:], a["wg"][0:128, :]).then_inc(S["w_in"], 16)
            for dst, s in ((SRC, "srcT"), (DST, "dstT"), (ETY, "etT"), (DSTG, "dstG"), (CST, "cst")):
                sp.dma_start(dst[:], a[s]).then_inc(S["edges_in"], 16)
            with sp.Fori(0, RT // 2) as i:
                for j in range(2):
                    t = i * 2 + j
                    sp.wait_ge(S["xn_done"], t + 1)
                    sp.dma_start(xn_rows[bass.ts(t, ROWS), :], ROW[:, 2 + j, :]).then_inc(S["xn_stored"], 16)
                    sp.wait_ge(S["xn_stored"], t * 16 + 16)
                    sp.sem_inc(S["xn_free"], 1)
            sp.wait_ge(S["zeros_made"], 1)
            sp.dma_start(inv_table[N * REL:(N + 1) * REL, :].rearrange("a b -> b a"), ZF[:]).then_inc(S["inv_zero"], 16)
            for L in range(2):
                sp.wait_ge(S["bias_free"], L + 1)
                sp.dma_start(BIAS[:], a["b1" if L == 0 else "b2"].broadcast_to([ROWS, D])).then_inc(S["bias_in"], 16)

                def store_messages(p, counts):
                    sp.wait_ge(S["w_lo"], p + ((REL + 1) * L + 1))
                    sp.dma_start(WST[:], a["wg"][bass.ts(p + ((REL + 1) * L + 1), 128), :]).then_inc(S["w_in"], 16)
                    with sp.Fori(0, RT // 2) as i:
                        for j in range(2):
                            t = i * 2 + j
                            sp.wait_ge(S["pair_out"], p * RT + t + (100 * L + 3))
                            sp.dma_start(msg_rows[bass.ts(t, ROWS), bass.ds(p, 1), :].rearrange("n r c -> n (r c)"),
                                         MSG[:, j, :]).then_inc(S["msg_out"], 16)
                            if counts:
                                sp.wait_ge(S["inv_made"], t + 3)
                                sp.dma_start(inv_table[bass.ts(t, ROWS * REL), :].rearrange("(p r) c -> p (r c)", r=REL),
                                             CNT[0:ROWS, j, :]).then_inc(S["inv_out"], 16)
                                sp.wait_ge(S["inv_out"], t * 16 + 16)
                                sp.sem_inc(S["inv_free"], 1)
                            sp.wait_ge(S["msg_out"], p * (16 * RT) + t * 16 + (L * 16 * REL * RT + 16))
                            sp.sem_inc(S["msg_free"], 1)

                if L == 0:
                    store_messages(0, True)
                with sp.Fori(1 - L, REL) as p:
                    store_messages(p, False)
                if L == 0:
                    sp.wait_ge(S["w_lo"], REL + 1)
                    sp.dma_start(WST[:], a["wg"][bass.ts(REL + 1, 128), :]).then_inc(S["w_in"], 16)
            sp.wait_ge(S["w_lo"], W_MIX)
            sp.dma_start(WST[:, 0:WM], a["wm"][0:128, :]).then_inc(S["w_in"], 16)
            with sp.Fori(0, RT // 2) as i:
                for j in range(2):
                    b = i * 2 + j
                    sp.wait_ge(S["pair_out"], b + (190 + 3))
                    sp.dma_start(gnn_rows[bass.ts(b, ROWS), :], ROW[:, j, :]).then_inc(S["gnn_out"], 16)
                    sp.wait_ge(S["gnn_out"], b * 16 + 16)
                    sp.sem_inc(S["row_free"], 1)
            sp.dma_start(RF[:].rearrange("p a m -> p (a m)"), a["rf"]).then_inc(S["rf_in"], 16)
            sp.dma_start(WPR[:], a["wmp"]).then_inc(S["wp_in"], 16)
            with sp.Fori(0, PAIRS - 1) as it:
                sp.wait_ge(S["w_lo"], it + (W_MIX + 1))
                sp.dma_start(WST[:, 0:WM], a["wm"][bass.ts(it + 1, 128), :]).then_inc(S["w_in"], 16)
            sp.wait_ge(S["w_lo"], W_LORA)
            sp.dma_start(WST[:, 0:WM], a["wa"]).then_inc(S["w_in"], 16)
            sp.wait_ge(S["mix_dve"], mix.taken(PAIRS - 1, "o12"))
            for n_, key in enumerate(("bmp", "gamma", "beta")):
                sp.dma_start(VEC[:, n_, :], a[key].broadcast_to([ROWS, D])).then_inc(S["vec_in"], 16)

            def load_join(i):
                for j in range(2):
                    t = i * 2 + j
                    sp.wait_ge(S["jr_free"], t + 1)
                    for n_, rows in enumerate((xn_rows, a["x"], gnn_rows)):
                        sp.dma_start(JR[:, j, n_, :], rows[bass.ts(t, ROWS), :]).then_inc(S[f"jr_in{j}"], 16)

            def store_x2(i):
                for j in range(2):
                    t = i * 2 + j
                    sp.wait_ge(S["x2_made"], t + 1)
                    sp.dma_start(x2_rows[bass.ts(t, ROWS), :], ROW[:, j, :]).then_inc(S["x2_out"], 16)
                    sp.wait_ge(S["x2_out"], t * 16 + 16)
                    sp.sem_inc(S["x2_free"], 1)

            load_join(0)
            with sp.Fori(0, RT // 2 - 1) as i:
                load_join(i + 1)
                store_x2(i)
            store_x2(RT // 2 - 1)
            sp.dma_start(BAG[:], a["bag"].broadcast_to([ROWS, LW + EXPERTS])).then_inc(S["lg_in"], 16)
            sp.dma_start(TRI[:], a["tri"]).then_inc(S["lg_in"], 16)
            sp.wait_ge(S["w_lo"], W_LORA + 1)
            sp.dma_start(WST[:, 0:WF], a["wf"][0:128, :]).then_inc(S["w_in"], 16)
            with sp.Fori(0, PAIRS - 1) as it:
                sp.wait_ge(S["w_lo"], it + (W_FFN + 1))
                sp.dma_start(WST[:, 0:WF], a["wf"][bass.ts(it + 1, 128), :]).then_inc(S["w_in"], 16)
            sp.wait_ge(S["w_lo"], W_OUT)
            sp.dma_start(WST[:, 0:WF], a["wf"][(PAIRS - 1) * 128:PAIRS * 128, :]).then_inc(S["w_in"], 16)
            sp.wait_ge(S["w_lo"], W_OUT + 1)
            sp.dma_start(WST[:], a["wo"]).then_inc(S["wp_in"], 16)
            sp.wait_ge(S["ffn_dve"], ffn.taken(PAIRS - 1, "O12"))
            sp.dma_start(OB[:], a["bo"].broadcast_to([ROWS, D])).then_inc(S["ob_in"], 16)
            with sp.Fori(0, RT // 2) as i:
                for j in range(2):
                    t = i * 2 + j
                    sp.wait_ge(S["or_free"], t + 1)
                    sp.dma_start(OR[:, j, :], x2_rows[bass.ts(t, ROWS), :]).then_inc(S[f"or_in{j}"], 16)
                for j in range(2):
                    t = i * 2 + j
                    sp.wait_ge(S["fp_free"], t + 3)
                    sp.dma_start(out[bass.ts(t, ROWS), :], ROW[:, j, :]).then_inc(S["out_out"], 16)
                    sp.wait_ge(S["out_out"], t * 16 + 16)
                    sp.sem_inc(S["out_free"], 1)
            sp.wait_ge(S["out_out"], 16 * RT)

        @block.gpsimd
        def _(g):

            def scale(q):
                g.wait_ge(S["w_max"], q + 1)
                g.sem_inc(S["pool_tick"], 1)
                g.partition_all_reduce(SC[:, POW], SC[:, PPOW], 128, bass.bass_isa.ReduceOp.max)
                g.drain()
                g.tensor_scalar(SC[:, POW], SC[:, POW], TINY, None, ALU.max)
                g.drain()
                g.tensor_scalar(SCI[:, WSCALE], SCI[:, POW], -1.0, float((254 + TOP) << 23), ALU.mult, ALU.add)
                g.tensor_scalar(SC[:, WINV], SC[:, POW], 2.0 ** -TOP, None, ALU.mult)
                g.tensor_scalar(SC[:, XWINV], SC[:, POW], 2.0 ** -TOP / X_SCALE, None, ALU.mult)
                g.drain()
                g.sem_inc(S["w_scale"], 1)

            def gather_weights(i):
                g.tensor_copy(IDXW[:], DKEY[:, bass.ts(i, BATCH)])
                g.drain()
                for j in range(BATCH):
                    g.indirect_dma_start(out=WGTW[:, j:j + 1], out_offset=None, in_=inv_table,
                                         in_offset=bass.IndirectOffsetOnAxis(ap=IDXW[:, j:j + 1], axis=0)).then_inc(S["wgt_in"], 16)
                g.wait_ge(S["wgt_in"], i * (16 * BATCH) + 16 * BATCH)
                g.tensor_copy(WALL[:, bass.ts(i, BATCH)], WGTW[:]).then_inc(S["wgt_done"], 1)
                g.drain()

            scale(0)
            scale(1)
            g.wait_ge(S["inv_out"], 16 * RT)
            g.wait_ge(S["inv_zero"], 16)
            with g.Fori(0, REL) as p:
                gather_weights(p)
                scale(p + 2)
            cnt = g.alloc_register("g_groups")
            g.reg_mov(cnt, 0)
            for L in range(2):
                if L == 1:
                    with g.Fori(0, REL) as p:
                        scale(p + REL + 2)
                if L == 1:
                    scale(W_MIX)
                g.wait_ge(S["msg_out"], 16 * REL * RT * (L + 1))
                with g.Fori(0, RT) as b:
                    lo = g.value_load(LIM[0:1, bass.ts(b, 1)], min_val=0, max_val=GROUPS - 1)
                    hi = g.value_load(LIM[0:1, bass.ds(b + RT, 1)], min_val=1, max_val=GROUPS)
                    with g.Fori(lo, hi) as e:
                        n = g.snap(cnt, min_val=0, max_val=1 << 20)
                        for j in range(GRP):
                            g.wait_ge(S["idx_made"], n * GRP + (j + 1))
                            g.sem_inc(S["pool_tick"], 1)
                            g.indirect_dma_start(out=GAT[:, j, :], out_offset=None, in_=msg_table,
                                                 in_offset=bass.IndirectOffsetOnAxis(ap=IDXG[:, j:j + 1], axis=0)).then_inc(S[f"gat_in{j}"], 16)
                        g.reg_add(cnt, cnt, 1)
            with g.Fori(0, PAIRS) as it:
                scale(it + (W_MIX + 1))
            g.wait_ge(S["vec_in"], 3 * 16)
            with g.Fori(0, RT // 2) as i:
                for j in range(2):
                    g.wait_ge(S[f"jr_in{j}"], i * 48 + 48)
                    g.sem_inc(S["pool_tick"], 1)
                    g.wait_ge(S["jp_free"], i * 2 + (j + 1))
                    g.sem_inc(S["pool_tick"], 1)
                    jp = JP[:, bass.ds((i % 2) * 2 + j, 1), :, :].rearrange("p a n c -> p (a n) c")
                    g.tensor_tensor(jp[:, 0, :], JR[:, j, 0, :], VEC[:, 0, :], ALU.add)
                    g.tensor_tensor(JR[:, j, 1, :], JR[:, j, 1, :], JR[:, j, 2, :], ALU.add)
                    g.drain()
                    g.tensor_tensor(jp[:, 1, :], JR[:, j, 1, :], VEC[:, 2, :], ALU.add)
                    g.drain()
                    g.sem_inc(S["jr_made"], 1)
                    g.sem_inc(S["jr_free"], 1)
            scale(W_FFN)
            g.wait_ge(S["lt_max"], 1)
            g.sem_inc(S["pool_tick"], 1)
            g.partition_all_reduce(QK[:, LALL], QK[:, LPOW], 128, bass.bass_isa.ReduceOp.max).then_inc(S["lt_pow"], 1)
            with g.Fori(0, PAIRS) as it:
                for n_ in range(2 * 3 * RT):
                    h, c, t = n_ // 30, n_ // 10 % 3, n_ % 10
                    n = CHUNKS[c][1]
                    if n_ == SPLIT_AT - 4:
                        scale(it + (W_FFN + 1))
                    g.wait_ge(S["ffn_act"], ffn.taken(it, f"S{h}{c}{t}"))
                    g.sem_inc(S["pool_tick"], 1)
                    g.tensor_tensor(P2[:, n_ % PARTED, 1, 0:n], PF[:, n_ % EXPS, 0:n], P2[:, n_ % PARTED, 0, 0:n], ALU.subtract).then_inc(S["ffn_lo"], 1)
            g.wait_ge(S["ob_in"], 16)
            with g.Fori(0, RT // 2) as i:
                for j in range(2):
                    g.wait_ge(S[f"or_in{j}"], i * 16 + 16)
                    g.sem_inc(S["pool_tick"], 1)
                    g.tensor_tensor(OR[:, j, :], OR[:, j, :], OB[:], ALU.add).then_inc(S["or_made"], 1)

        @block.scalar
        def _(act):
            act.wait_ge(S["stat_done"], 1)
            act.activation(LNR[:, 1, :], LNR[:, 0, :], ACT.Sqrt).then_inc(S["sd_done"], 1)
            with act.Fori(0, RT // 2) as i:
                for j in range(2):
                    t = i * 2 + j
                    act.wait_ge(S["xt_made"], t + 1)
                    act.activation(xtview(XT, 0, t), tview(2 * j), ACT.Copy, scale=X_SCALE).then_inc(S["t_hi"], 1)

            def split_high(q, done=None, W=WHL, cols=KT * D):
                if done is not None:
                    act.wait_ge(S["acc_done"], done)
                act.wait_ge(S["w_scale"], q + 1)
                act.activation(W[:, bass.ds(q % 2, 1), 0, 0:cols].rearrange("p a c -> p (a c)"), WST[:, 0:cols], ACT.Copy,
                               scale=SC[:, WSCALE]).then_inc(S["w_hi"], 1)

            split_high(0, 1)
            for L in range(2):
                with act.Fori(0, REL) as p:
                    split_high(p + ((REL + 1) * L + 1), p * RT + (100 * L + 1))
                if L == 0:
                    split_high(REL + 1, REL * RT + 1)
                if L == 0:
                    def relu(b, j):
                        act.wait_ge(S["h_scale"], b + 1)
                        act.wait_ge(S["h_free"], b + 1)
                        act.activation(ROW[:, 2 + j, :], ROW[:, j, :], ACT.Relu, scale=HMX[:, j, 2:3]).then_inc(S["relu_made"], 1)

                    def h_high(b, j):
                        act.wait_ge(S["h_t"], b + 1)
                        act.activation(xtview(HT, 0, b), tview(4 + 2 * j), ACT.Copy).then_inc(S["h_hi"], 1)

                    relu(0, 0)
                    with act.Fori(0, RT // 2 - 1) as i:
                        relu(i * 2 + 1, 1)
                        h_high(i * 2, 0)
                        relu(i * 2 + 2, 0)
                        h_high(i * 2 + 1, 1)
                    relu(RT - 1, 1)
                    h_high(RT - 2, 0)
                    h_high(RT - 1, 1)
            split_high(W_MIX, 100 + 80 + 1, WHM, WM)
            with act.Fori(0, PAIRS) as it:
                for T, x in ((QA, "q"), (KA, "k")):
                    for c, (c0, n) in enumerate(CHUNKS):
                        act.wait_ge(S["mix_pe"], mix.made(it, f"{x}{c}"))
                        p = PS[:, mix.bank(f"{x}{c}"), 0:n]
                        up, down = SC[0:64, XWINV], SC[64:128, XWINV]
                        act.activation(T[0:64, 0, c0:c0 + n], p[0:64, :], ACT.Copy, scale=up)
                        act.activation(T[64:128, 1, c0:c0 + n], p[64:128, :], ACT.Copy, scale=down)
                        act.activation(T[64:128, 0, c0:c0 + n], p[0:64, :], ACT.Square, scale=up)
                        act.activation(T[0:64, 1, c0:c0 + n], p[64:128, :], ACT.Square, scale=down).then_inc(S["mix_act"], 1)
                for h in range(2):
                    for u in range(RT // 2):
                        act.wait_ge(S["mix_pe"], mix.made(it, f"K{h}{u}"))
                        act.activation(KP[:, 2 * u:2 * u + 2, :].rearrange("p t m -> p (t m)"), PS[0:ROWS, mix.bank(f"K{h}{u}"), :], ACT.Exp).then_inc(S["mix_act"], 1)
                    if h == 1:
                        split_high(it + (W_MIX + 1), W=WHM, cols=WM)
                    for m in range(2):
                        for c, (c0, n) in enumerate(CHUNKS):
                            act.wait_ge(S["mix_pe"], mix.made(it, f"Q{h}{m}{c}"))
                            act.activation(QP[:, m, c0:c0 + n], PS[:, mix.bank(f"Q{h}{m}{c}"), 0:n], ACT.Exp).then_inc(S["mix_act"], 1)
            with act.Fori(0, RT // 2) as i:
                for k in range(2):
                    act.wait_ge(S["js_done"], i * 2 + (k + 1))
                    act.activation(STAT[:, :, 15], STAT[:, :, 14], ACT.Sqrt).then_inc(S["js_sd"], 1)
                for j in range(2):
                    t = i * 2 + j
                    act.wait_ge(S["xf_t"], t + 1)
                    act.activation(xtview(XT, 0, t), tview(4 + 2 * j), ACT.Copy, scale=X_SCALE).then_inc(S["xf_hi"], 1)
            split_high(W_FFN, W=WHM, cols=WM)
            act.wait_ge(S["gate_in"], 1)
            act.activation(GP[:, 1], GP[:, 0], ACT.Exp).then_inc(S["gate_ex"], 1)
            for u in range(RT // 2):
                act.wait_ge(S["lt_pe"], u + 1)
                act.activation(LT[:, :, 2 * u * ROWS:2 * (u + 1) * ROWS], PS[:, 2 + u, 0:4 * ROWS].rearrange("p (k c) -> p k c", k=2), ACT.Copy,
                               scale=X_SCALE).then_inc(S["lt_free"], 1)
            act.wait_ge(S["qk_scale"], 1)
            with act.Fori(0, PAIRS) as it:
                for x, T in (("q", QS), ("k", KS)):
                    for c, (c0, n) in enumerate(CHUNKS):
                        act.wait_ge(S["ffn_pe"], ffn.made(it, f"{x}{c}"))
                        p = PS[:, ffn.bank(f"{x}{c}"), 0:n]
                        for h in range(2):
                            rows = slice(64 * h, 64 * h + 64)
                            for to in (rows, slice(64 - 64 * h, 128 - 64 * h))[:2 if x == "q" else 1]:
                                ins = act.activation(T[to, h, c0:c0 + n], p[rows, :], ACT.Copy, scale=QK[rows, QKS])
                        ins.then_inc(S["ffn_hi"], 1)
                for c in range(3):
                    t0, t1 = 4 * c, min(4 * c + 4, RT)
                    act.wait_ge(S["ffn_pe"], ffn.made(it, f"v{c}"))
                    act.activation(V2[:, 0, t0:t1, :, 0:64], PS[0:ROWS, ffn.bank(f"v{c}"), 0:(t1 - t0) * 128]
                                   .rearrange("p (t h d) -> p t h d", h=2, d=DH), ACT.Copy, scale=SC[0:ROWS, XWINV]).then_inc(S["ffn_hi"], 1)
                act.wait_ge(S["s_scale"], it + 1)
                for s_ in range(RT):
                    act.wait_ge(S["ffn_dve"], ffn.taken(it, f"M0{s_}"))
                    act.activation(DG[:, 0, s_ * ROWS:(s_ + 1) * ROWS], IDB[0:ROWS, 0:ROWS], ACT.Copy, scale=NM[:, 0, s_:s_ + 1]).then_inc(S["dg0_made"], 1)
                for n_ in range(2 * 3 * RT):
                    h, c, t = n_ // 30, n_ // 10 % 3, n_ % 10
                    n = CHUNKS[c][1]
                    p = PS[0:ROWS, ffn.bank(f"S{h}{c}{t}"), 0:n]
                    if n_ == SPLIT_AT:
                        split_high(it + (W_FFN + 1), W=WHM, cols=WM)
                    act.wait_ge(S["ffn_pe"], ffn.made(it, f"S{h}{c}{t}"))
                    act.wait_ge(S["ffn_lo"], it * 60 + (n_ + 1))
                    act.activation(PF[:, n_ % EXPS, 0:n], p, ACT.Exp, scale=QK[0:ROWS, SSCALE])
                    act.wait_ge(S["av_done"], it * 60 + (n_ + 1))
                    act.activation(P2[:, n_ % PARTED, 0, 0:n], p, ACT.Exp, scale=QK[0:ROWS, SSCALE]).then_inc(S["ffn_act"], 1)

        @block.vector
        def _(v):
            v.memset(ZERO[:], 0.0).then_inc(S["zeros_made"], 1)
            v.memset(ZF[:], 0.0)
            v.drain()
            v.sem_inc(S["t_free"], 2)
            for n_, k_ in (("xn_free", 2), ("acc_done", 1), ("pair_out", 2), ("msg_free", 2), ("bias_free", 1), ("hot1_used", RING),
                           ("edge_used", GRP), ("h_free", 2), ("row_free", 2), ("mix_act", mix.size["act"]), ("mix_dve", mix.size["dve"]), ("mp_free", 2), ("jr_free", 2), ("jp_free", 4),
                           ("x2_free", 2), ("lg_free", 2), ("ffn_dve", ffn.size["dve"]), ("ffn_act", ffn.size["act"]), ("ffn_lo", EXPS), ("av_done", PARTED),
                           ("or_free", 2), ("fp_free", 2), ("out_free", 2),  ("xf_free", 2), ("inv_free", 2), ("inv_made", 2)):
                v.sem_inc(S[n_], k_)

            def panel_max(q, cols=KT * D):
                v.wait_ge(S["w_in"], q * 16 + 16)
                v.tensor_reduce(SC[:, PMAX], WST[:, 0:cols], AX.X, ALU.max, apply_absolute_value=True)
                v.drain()
                v.tensor_scalar(SCI[:, PPOW], SCI[:, PMAX], EXPONENT, None, ALU.bitwise_and).then_inc(S["w_max"], 1)

            def split_low(q, W=WHL, cols=KT * D, ranks=False):
                v.wait_ge(S["w_hi"], q + 1)
                if ranks:
                    v.tensor_scalar(F67[:], WST[:, WM:WF], SC[:, WSCALE], None, ALU.mult)
                    v.drain()
                v.scalar_tensor_tensor(W[:, bass.ds(q % 2, 1), 1, 0:cols].rearrange("p a c -> p (a c)"), WST[:, 0:cols], SC[:, WSCALE],
                                       W[:, bass.ds(q % 2, 1), 0, 0:cols].rearrange("p a c -> p (a c)"), ALU.mult, ALU.subtract).then_inc(S["w_lo"], 1)

            def newton(var, sd, r, e):
                v.reciprocal(r, sd)
                v.drain()
                v.tensor_tensor(e, r, r, ALU.mult)
                v.drain()
                v.tensor_tensor(e, e, var, ALU.mult)
                v.drain()
                v.tensor_scalar(e, e, -0.5, 1.5, ALU.mult, ALU.add)
                v.drain()
                v.tensor_tensor(r, r, e, ALU.mult)
                v.drain()

            for t in range(RT):
                if t in (0, RT // 2):
                    v.wait_ge(S[f"x_in{2 * t // RT}"], 16)
                for h in range(2):
                    v.bn_stats(LNS[:, t, 6 * h:6 * h + 6], ROOT[:, t, h * HALF:(h + 1) * HALF])
            v.drain()
            for t in range(RT):
                v.bn_aggr(LNS[:, t, 12:14], LNS[:, t, 0:12])
            v.drain()
            v.tensor_scalar(LNR[:, 0, :], LNS[:, :, 13], LN_EPS, None, ALU.add).then_inc(S["stat_done"], 1)
            panel_max(0)
            v.wait_ge(S["sd_done"], 1)
            newton(*(LNR[:, n_, :] for n_ in range(4)))
            with v.Fori(0, RT // 2) as i:
                for j in range(2):
                    t = i * 2 + j
                    v.wait_ge(S["t_free"], t + 1)
                    v.wait_ge(S["xn_free"], t + 1)
                    v.tensor_scalar(ROW[:, 2 + j, :], ROOT[:, bass.ts(t, 1), :].rearrange("p a c -> p (a c)"), LNS[:, bass.ts(t, 1), 12:13].rearrange("p a c -> p (a c)"),
                                    LNR[:, 2, bass.ts(t, 1)], ALU.subtract, ALU.mult).then_inc(S["xn_done"], 1)
                for j in range(2):
                    t = i * 2 + j
                    v.wait_ge(S["t_hi"], t + 1)
                    v.scalar_tensor_tensor(xtview(XT, 1, t), tview(2 * j), X_SCALE, xtview(XT, 0, t), ALU.mult, ALU.subtract).then_inc(S["t_free"], 1)
            v.drain()
            v.wait_ge(S["edges_in"], 5 * 16)
            v.tensor_copy(DSTF[:], DST[:])
            v.tensor_copy(ETF[:], ETY[:])
            v.tensor_copy(TMPF[:], SRC[:])
            v.tensor_copy(IOTA[:], CST[:, 0:128])
            v.drain()
            v.scalar_tensor_tensor(SKEY[:], TMPF[:], float(REL), ETF[:], ALU.mult, ALU.add)
            v.memset(DKEY[:, TILES:], 0)
            v.scalar_tensor_tensor(DKEY[:, 0:TILES], DSTF[:], float(REL), ETF[:], ALU.mult, ALU.add)
            v.tensor_tensor(TYPEHOT[:], ETF[:].unsqueeze(2).broadcast_to([128, TILES, REL]),
                            IOTA[:, 0:REL].unsqueeze(1).broadcast_to([128, TILES, REL]), ALU.is_equal)
            split_low(0)
            v.tensor_reduce(GB[:, 0:1], DSTG[:], AX.X, ALU.min)
            v.tensor_reduce(GB[:, 1:2], DSTG[:], AX.X, ALU.max)
            v.drain()
            lbs, ubs, up, down = (CST[0:GROUPS, 128:138], CST[0:GROUPS, 138:148], CST[0:GROUPS, 148:149], CST[0:GROUPS, 149:150])
            v.tensor_scalar(GB[:, 4:14], lbs, GB[:, 1:2], None, ALU.is_le)
            v.tensor_scalar(GB[:, 14:24], ubs, GB[:, 0:1], None, ALU.is_gt)
            v.drain()
            v.tensor_tensor(GB[:, 24:34], GB[:, 4:14], GB[:, 14:24], ALU.mult)
            v.drain()
            v.tensor_scalar(GB[:, 40:50], GB[:, 24:34], down, None, ALU.mult)
            v.tensor_scalar(GB[:, 50:60], GB[:, 24:34], up, None, ALU.mult)
            v.drain()
            v.sem_inc(S["bounds_made"], 1)
            v.wait_ge(S["bounds_t"], 1)
            v.tensor_reduce(LIMR[:, 0:1], PS[0:2 * RT, 0, 0:GROUPS], AX.X, ALU.max).then_inc(S["lim_row"], 1)
            v.wait_ge(S["lim_t"], 1)
            v.tensor_scalar(LIMF[:, 0:RT], PS[0:1, 1, 0:RT], -1.0, float(GROUPS), ALU.mult, ALU.add)
            v.drain()
            v.tensor_scalar(LIMF[:, 2 * RT:3 * RT], LIMF[:, 0:RT], float(GROUPS - 1), None, ALU.min)
            v.drain()
            v.tensor_scalar(LIMF[:, 0:RT], LIMF[:, 2 * RT:3 * RT], 1.0, None, ALU.add)
            v.drain()
            v.tensor_tensor(LIMF[:, 3 * RT:4 * RT], LIMF[:, 0:RT], PS[0:1, 1, RT:2 * RT], ALU.max)
            v.drain()
            v.tensor_copy(LIM[:], LIMF[:, 2 * RT:4 * RT])
            v.drain()
            v.sem_inc(S["lim_made"], 1)

            v.memset(ROWINV[:], 1.0 / X_SCALE)
            cnt = v.alloc_register("v_groups")
            v.reg_mov(cnt, 0)

            def one_hot_rows(b):
                v.drain()
                v.tensor_scalar(DLOC[:], DSTF[:], CST[:, bass.ds(b + 128, 1)], None, ALU.subtract)
                v.drain()
                lo, hi = block_bounds(v, b)
                with v.Fori(lo, hi) as e:
                    n = v.snap(cnt, min_val=0, max_val=1 << 20)
                    slot = v.snap((n % RING) * GRP, min_val=0, max_val=(RING - 1) * GRP)
                    v.wait_ge(S["hot1_used"], n + 1)
                    v.tensor_tensor(HOTC[:, bass.ds(slot, GRP), :], IOTA[:, 0:ROWS].unsqueeze(1).broadcast_to([128, GRP, ROWS]),
                                    DLOC[:, bass.ds(e * GRP, GRP)].unsqueeze(2).broadcast_to([128, GRP, ROWS]),
                                    ALU.is_equal).then_inc(S["hot1_made"], 1)
                    v.reg_add(cnt, cnt, 1)

            def inverse_counts(b, j):
                v.wait_ge(S["cnt_done"], b + 1)
                v.wait_ge(S["inv_free"], b + 1)
                v.tensor_scalar(CNT[0:ROWS, j, :], PS[0:ROWS, 4 + j, 0:REL], 1.0, None, ALU.max)
                v.drain()
                v.reciprocal(CNT[0:ROWS, j, :], CNT[0:ROWS, j, :])
                v.drain()
                v.sem_inc(S["inv_made"], 1)

            for L in range(2):
                def out_scales(q):
                    v.drain()
                    v.wait_ge(S["w_lo"], q + 1)
                    v.tensor_scalar(OUTINV[:], ROWINV[:], SC[0:ROWS, WINV], None, ALU.mult)
                    v.drain()

                def messages(p, counts):
                    q = p + (REL + 1) * L
                    out_scales(q)
                    for part in PARTS:
                        with v.Fori(*part) as i:
                            for j in range(2):
                                t = i * 2 + j
                                if counts:
                                    one_hot_rows(t)
                                v.wait_ge(S["acc_done"], p * RT + t + (100 * L + 2))
                                v.wait_ge(S["msg_free"], p * RT + t + (REL * RT * L + 1))
                                v.tensor_scalar(halves(MSG[:, j, :]), rowps(2 * j), OUTINV[:, bass.ts(t, 1)], None, ALU.mult).then_inc(S["pair_out"], 1)
                                if counts:
                                    inverse_counts(t, j)
                        if part == PARTS[0]:
                            panel_max(q + 1)
                        elif part == PARTS[1]:
                            split_low(q + 1)

                if L == 0:
                    messages(0, True)
                    v.reg_mov(cnt, 0)
                with v.Fori(1 - L, REL) as p:
                    messages(p, False)
                v.wait_ge(S["bias_in"], 16 * (L + 1))
                out_scales((REL + 1) * L + REL)
                for part in PARTS:
                    with v.Fori(*part) as i:
                        for j in range(2):
                            t = i * 2 + j
                            v.wait_ge(S["acc_done"], t + (100 * L + 80 + 2))
                            v.scalar_tensor_tensor(halves(ROOT[:, bass.ts(t, 1), :].rearrange("p a c -> p (a c)")), rowps(2 * j), OUTINV[:, bass.ts(t, 1)],
                                                   halves(BIAS[:]), ALU.mult, ALU.add).then_inc(S["pair_out"], 1)
                    if part == PARTS[0]:
                        panel_max((REL + 1) * (L + 1), KT * D if L == 0 else WM)
                    elif part == PARTS[1]:
                        split_low((REL + 1) * (L + 1), *((WHL, KT * D) if L == 0 else (WHM, WM)))
                v.drain()
                v.sem_inc(S["bias_free"], 1)
                if L == 0:
                    v.wait_ge(S["wgt_done"], REL)
                def weighted_rows(b):
                    v.drain()
                    v.tensor_scalar(DLOC[:], DSTF[:], CST[:, bass.ds(b + 128, 1)], None, ALU.subtract)
                    v.drain()
                    lo, hi = block_bounds(v, b)
                    with v.Fori(lo, hi) as e:
                        n = v.snap(cnt, min_val=0, max_val=1 << 20)
                        for k in range(GRP):
                            v.wait_ge(S["edge_used"], n * GRP + (k + 1))
                            v.tensor_copy(IDXG[:, k:k + 1], SKEY[:, bass.ds(e * GRP + k, 1)]).then_inc(S["idx_made"], 1)
                            v.tensor_scalar(HOT[:, k, :], IOTA[:, 0:ROWS], DLOC[:, bass.ds(e * GRP + k, 1)],
                                            WALL[:, bass.ds(e * GRP + k, 1)], ALU.is_equal, ALU.mult).then_inc(S["hot_made"], 1)
                        v.reg_add(cnt, cnt, 1)

                def block_out(b, j):
                    v.wait_ge(S["acc_done"], b + (100 * L + 90 + 2))
                    if L == 1:
                        v.wait_ge(S["row_free"], b + 1)
                    v.tensor_tensor(halves(ROW[:, j, :]), rowps(2 * j),
                                    halves(ROOT[:, bass.ts(b, 1), :].rearrange("p a c -> p (a c)")), ALU.add).then_inc(S["pair_out"], 1)
                    if L == 0:
                        v.drain()
                        v.tensor_reduce(HMX[:, j, 0:1], ROW[:, j, :], AX.X, ALU.max)
                        v.drain()
                        v.tensor_scalar(HMX[:, j, 0:1], HMX[:, j, 0:1], TINY, None, ALU.max)
                        v.drain()
                        v.tensor_scalar(HMXI[:, j, 1:2], HMXI[:, j, 0:1], EXPONENT, None, ALU.bitwise_and)
                        v.drain()
                        v.tensor_scalar(HMXI[:, j, 2:3], HMXI[:, j, 1:2], -1.0, float((254 + TOP) << 23), ALU.mult, ALU.add)
                        v.tensor_scalar(ROWINV[:, bass.ts(b, 1)], HMX[:, j, 1:2], 2.0 ** -TOP, None, ALU.mult)
                        v.drain()
                        v.sem_inc(S["h_scale"], 1)

                def h_low(b, j):
                    if L == 0:
                        v.wait_ge(S["h_hi"], b + 1)
                        v.tensor_tensor(xtview(HT, 1, b), tview(4 + 2 * j), xtview(HT, 0, b), ALU.subtract).then_inc(S["h_free"], 1)

                for b in range(3):
                    weighted_rows(b)
                    if b:
                        block_out(b - 1, (b - 1) % 2)
                with v.Fori(0, (RT - 4) // 2) as i:
                    for j in range(2):
                        b = i * 2 + (3 + j)
                        weighted_rows(b)
                        h_low(i * 2 + j, j)
                        block_out(i * 2 + (2 + j), j)
                weighted_rows(RT - 1)
                h_low(RT - 4, 0)
                block_out(RT - 2, 0)
                h_low(RT - 3, 1)
                block_out(RT - 1, 1)
                h_low(RT - 2, 0)
                h_low(RT - 1, 1)
            v.drain()
            v.memset(VA[:, :, :, 64:128], 1.0).then_inc(S["ones_made"], 1)

            def normalise(psum, n, c0, it, h):
                r, o = RCPF[:, 0, 0:n], HF[64 * h:64 * h + 64, bass.ds(it, 1), c0:c0 + n].rearrange("p a c -> p (a c)")
                v.reciprocal(r, psum[64:128, 0:n])
                v.drain()
                return v.tensor_tensor(o, psum[0:64, 0:n], r, ALU.mult)

            with v.Fori(0, PAIRS) as it:
                for c in range(3):
                    t0, t1 = 4 * c, min(4 * c + 4, RT)
                    v.wait_ge(S["mix_pe"], mix.made(it, f"v{c}"))
                    v.tensor_scalar(VA[:, t0:t1, :, 0:64], PS[0:ROWS, mix.bank(f"v{c}"), 0:(t1 - t0) * 128]
                                    .rearrange("p (t h d) -> p t h d", h=2, d=DH), SC[0:ROWS, XWINV], None, ALU.mult).then_inc(S["mix_dve"], 1)
                v.wait_ge(S["mix_act"], mix.taken(it, "k2"))
                panel_max(it + (W_MIX + 1), WM)

                def take_kv(h):
                    v.wait_ge(S["mix_pe"], mix.made(it, f"kv{h}"))
                    v.tensor_scalar(KV[:].rearrange("p m d -> p (m d)"), PS[:, mix.bank(f"kv{h}"), 0:256], 1.0 / MF, None, ALU.mult).then_inc(S["mix_dve"], 1)

                def take_outputs(h):
                    for c, (c0, n) in enumerate(CHUNKS):
                        v.wait_ge(S["mix_pe"], mix.made(it, f"o{h}{c}"))
                        v.tensor_scalar(RCP[64 * h:64 * h + 64, c0:c0 + n], PS[64:128, mix.bank(f"o{h}{c}"), 0:n], 1e-6, None, ALU.add)
                        v.tensor_copy(NUM[64 * h:64 * h + 64, c0:c0 + n], PS[0:64, mix.bank(f"o{h}{c}"), 0:n]).then_inc(S["mix_dve"], 1)
                    v.drain()

                take_kv(0)
                take_outputs(0)
                split_low(it + (W_MIX + 1), WHM, WM)
                take_kv(1)
                take_outputs(1)
                v.reciprocal(RCP[:], RCP[:])
                v.drain()
                v.tensor_tensor(HF[:, bass.ds(it, 1), :].rearrange("p a c -> p (a c)"), NUM[:], RCP[:], ALU.mult).then_inc(S["hf_made"], 1)
                v.drain()

            def pair_statistics(nth):
                for j in range(2):
                    for h in range(2):
                        v.bn_stats(STAT[:, j, 6 * h:6 * h + 6], ROW[:, j, h * HALF:(h + 1) * HALF])
                v.drain()
                for j in range(2):
                    v.bn_aggr(STAT[:, j, 12:14], STAT[:, j, 0:12])
                v.drain()
                v.tensor_scalar(STAT[:, :, 14], STAT[:, :, 13], LN_EPS, None, ALU.add).then_inc(S["js_done"], 1)
                v.wait_ge(S["js_sd"], nth)
                newton(*(STAT[:, :, n_] for n_ in (14, 15, 16, 17)))

            def normalised(out, j):
                return v.tensor_scalar(out, ROW[:, j, :], STAT[:, j, 12:13], STAT[:, j, 16:17], ALU.subtract, ALU.mult)

            with v.Fori(0, RT // 2) as i:
                jp = lambda j: JP[:, bass.ds((i % 2) * 2 + j, 1), :, :].rearrange("p a n c -> p (a n) c")
                for j in range(2):
                    t = i * 2 + j
                    v.wait_ge(S["mp_done"], t + 1)
                    v.wait_ge(S["jr_made"], t + 1)
                    v.wait_ge(S["x2_free"], t + 1)
                    v.tensor_tensor(halves(ROW[:, j, :]), rowps(2 * j), halves(jp(j)[:, 0, :]), ALU.add).then_inc(S["mp_free"], 1)
                v.drain()
                pair_statistics(i * 2 + 1)
                for j in range(2):
                    normalised(ROW[:, j, :], j)
                v.drain()
                for j in range(2):
                    v.tensor_tensor(ROW[:, j, :], ROW[:, j, :], VEC[:, 1, :], ALU.mult)
                v.drain()
                for j in range(2):
                    v.tensor_tensor(ROW[:, j, :], ROW[:, j, :], jp(j)[:, 1, :], ALU.add).then_inc(S["x2_made"], 1)
                v.drain()
                v.sem_inc(S["jp_free"], 2)
                pair_statistics(i * 2 + 2)
                for j in range(2):
                    v.wait_ge(S["xf_free"], i * 2 + (j + 1))
                    normalised(ROW[:, 2 + j, :], j).then_inc(S["xf_made"], 1)
                for j in range(2):
                    t = i * 2 + j
                    v.wait_ge(S["xf_hi"], t + 1)
                    v.scalar_tensor_tensor(xtview(XT, 1, t), tview(4 + 2 * j), X_SCALE, xtview(XT, 0, t), ALU.mult, ALU.subtract).then_inc(S["xf_free"], 1)
            v.drain()
            v.memset(HG[:], 0.0)
            v.memset(QK[:], 0.0)
            v.drain()
            v.memset(HG[:, :, LW + EXPERTS:LW + EXPERTS + 1], 1.0)
            v.tensor_copy(IDB[:], IDF[:])
            v.memset(ONB[:], 1.0)
            v.memset(V2[:, 0, :, :, 64:128], 1.0)
            v.memset(V2[:, 1, :, :, 64:128], 0.0)
            v.drain()
            v.sem_inc(S["ffn_ready"], 1)
            v.wait_ge(S["lg_in"], 32)
            with v.Fori(0, RT // 2) as i:
                for j in range(2):
                    t = i * 2 + j
                    v.wait_ge(S["lg_pe"], t + 1)
                    v.scalar_tensor_tensor(HG[:, bass.ts(t, 1), 0:LW + EXPERTS].rearrange("p a c -> p (a c)"), PS[0:ROWS, j, 0:LW + EXPERTS],
                                           SC[0:ROWS, XWINV], BAG[:], ALU.mult, ALU.add).then_inc(S["lg_free"], 1)
            v.drain()
            panel_max(W_FFN, WF)
            over = lambda ap: ap.unsqueeze(2).broadcast_to([ROWS, RT, EXPERTS])
            LOG = HG[:, :, LW:LW + EXPERTS]
            v.tensor_reduce(GM[:, 0, :], LOG, AX.X, ALU.max)
            v.drain()
            v.tensor_tensor(GP[:, 0], LOG, over(GM[:, 0, :]), ALU.subtract).then_inc(S["gate_in"], 1)
            split_low(W_FFN, WHM, WM, ranks=True)
            v.wait_ge(S["gate_ex"], 1)
            v.tensor_reduce(GM[:, 0, :], GP[:, 1], AX.X, ALU.add)
            v.drain()
            v.reciprocal(GM[:, 1, :], GM[:, 0, :])
            v.drain()
            v.tensor_tensor(GP[:, 0], GP[:, 1], over(GM[:, 1, :]), ALU.mult)
            v.drain()
            sq = [ROWS, RT, EXPERTS, EXPERTS]
            mine, others = GP[:, 0].unsqueeze(3).broadcast_to(sq), GP[:, 0].unsqueeze(2).broadcast_to(sq)
            g4 = lambda k: GT[:, k].rearrange("p t (e f) -> p t e f", f=EXPERTS)
            v.tensor_tensor(g4(0), others, mine, ALU.is_gt)
            v.tensor_tensor(g4(1), others, mine, ALU.is_equal)
            v.drain()
            v.tensor_tensor(GT[:, 1], GT[:, 1], TRI[0:ROWS].unsqueeze(1).broadcast_to([ROWS, RT, EXPERTS * EXPERTS]), ALU.mult)
            v.drain()
            v.tensor_tensor(GT[:, 0], GT[:, 0], GT[:, 1], ALU.add)
            v.drain()
            v.tensor_reduce(GP[:, 1], g4(0), AX.X, ALU.add)
            v.drain()
            v.tensor_scalar(GP[:, 2], GP[:, 1], 2.0, 2.0, ALU.is_lt, ALU.mult)
            v.drain()
            v.tensor_tensor(LOG, GP[:, 2], GP[:, 0], ALU.mult)
            v.drain()
            v.tensor_tensor(HG[:, :, 0:LW].rearrange("p t (e r) -> p t e r", r=16), HG[:, :, 0:LW].rearrange("p t (e r) -> p t e r", r=16),
                            LOG.unsqueeze(3).broadcast_to([ROWS, RT, EXPERTS, 16]), ALU.mult).then_inc(S["gate_done"], 1)
            v.drain()
            v.tensor_reduce(QK[0:ROWS, LMAX], HG[:].rearrange("p t c -> p (t c)"), AX.X, ALU.max, apply_absolute_value=True)
            v.drain()
            v.tensor_scalar(QKI[:, LPOW], QKI[:, LMAX], EXPONENT, None, ALU.bitwise_and).then_inc(S["lt_max"], 1)
            v.wait_ge(S["lt_pow"], 1)
            v.tensor_scalar(QK[:, LALL], QK[:, LALL], 4.0, None, ALU.max)
            v.drain()
            v.reciprocal(QK[:, QKS], QK[:, LALL])
            v.tensor_scalar(QK[:, QKINV], QK[:, LALL], 2.0 ** 16, None, ALU.mult)
            v.drain()
            v.tensor_scalar(QK[:, QKS], QK[:, QKS], 2.0 ** -16, None, ALU.mult)
            v.drain()
            v.sem_inc(S["qk_scale"], 1)
            with v.Fori(0, PAIRS) as it:
                for n_, x in enumerate("qk"):
                    for c, (c0, n) in enumerate(CHUNKS):
                        v.wait_ge(S["ffn_hi"], it * 9 + (3 * n_ + c + 1))
                        for h in range(2):
                            rows, other = slice(64 * h, 64 * h + 64), slice(64 - 64 * h, 128 - 64 * h)
                            T, to = (QS, QL[rows, c0:c0 + n]) if x == "q" else (KS, KS[other, h, c0:c0 + n])
                            ins = v.scalar_tensor_tensor(to, PS[rows, ffn.bank(f"{x}{c}"), 0:n], QK[rows, QKS], T[rows, h, c0:c0 + n], ALU.mult, ALU.subtract)
                        ins.then_inc(S["ffn_dve"], 1)
                v.tensor_tensor(QK[:, SINV], SC[:, XWINV], QK[:, QKINV], ALU.mult)
                v.drain()
                v.tensor_scalar(QK[:, SSCALE], QK[:, SINV], QK[:, SINV], DH ** -0.5, ALU.mult, ALU.mult)
                v.drain()
                v.sem_inc(S["s_scale"], 1)

                def v_low(c):
                    t0, t1 = 4 * c, min(4 * c + 4, RT)
                    v.wait_ge(S["ffn_hi"], it * 9 + (6 + c + 1))
                    for t in range(t0, t1):
                        ins = v.scalar_tensor_tensor(V2[:, 1, t, :, 0:64], PS[0:ROWS, ffn.bank(f"v{c}"), (t - t0) * 128:(t - t0 + 1) * 128]
                                                     .rearrange("p (h d) -> p h d", d=DH), SC[0:ROWS, XWINV], V2[:, 0, t, :, 0:64], ALU.mult, ALU.subtract)
                    ins.then_inc(S["ffn_dve"], 1)

                for r in (r for r, e, _ in FFN if e == "dve" and r[0] in "vMO"):
                    if r[0] == "v":
                        v_low(int(r[1]))
                        continue
                    v.wait_ge(S["ffn_pe"], ffn.made(it, r))
                    h = int(r[1])
                    if r[0] == "M":
                        s_ = int(r[2])
                        v.tensor_reduce(NM[:, h, s_:s_ + 1], PS[0:ROWS, ffn.bank(r):ffn.bank(r) + 3, :].rearrange("p b c -> p (b c)")[:, 0:N], AX.X, ALU.max,
                                        negate=True).then_inc(S["ffn_dve"], 1)
                        v.drain()
                        if h == 0:
                            continue
                        v.tensor_scalar(DG[:, h, s_ * ROWS:(s_ + 1) * ROWS], IDB[0:ROWS, 0:ROWS], NM[:, h, s_:s_ + 1], None, ALU.mult).then_inc(S["dg1_made"], 1)
                        if r == "M19":
                            panel_max(it + (W_FFN + 1), WF)
                    else:
                        c0, n = CHUNKS[int(r[2])]
                        normalise(PS[:, ffn.bank(r), :], n, c0, it, h).then_inc(S["ffn_dve"], 1)
                        v.drain()
                        if r == "O10":
                            split_low(it + (W_FFN + 1), WHM, WM, ranks=True)
            with v.Fori(0, RT // 2) as i:
                for j in range(2):
                    t = i * 2 + j
                    v.wait_ge(S["fp_done"], t + 1)
                    v.wait_ge(S["or_made"], t + 1)
                    v.wait_ge(S["out_free"], t + 1)
                    v.tensor_tensor(halves(ROW[:, j, :]), rowps(2 * j), halves(OR[:, j, :]), ALU.add).then_inc(S["fp_free"], 1)
                    v.drain()
                    v.sem_inc(S["or_free"], 1)

        @block.tensor
        def _(pe):
            def six_transposes(b0, slot, S_done):
                for k in range(KT):
                    o = PS[:, b0 + k // 3, (k % 3) * ROWS:(k % 3 + 1) * ROWS]
                    ins = pe.transpose(o, ROW[:, slot, k * 128:(k + 1) * 128], IDF[0:ROWS, 0:ROWS])
                ins.then_inc(S_done, 1)

            pe.wait_ge(S["consts_in"], 16)
            with pe.Fori(0, RT // 2) as i:
                for j in range(2):
                    t = i * 2 + j
                    pe.wait_ge(S["xn_done"], t + 1)
                    pe.wait_ge(S["t_free"], t + 1)
                    six_transposes(2 * j, 2 + j, S["xt_made"])
            pe.wait_ge(S["t_free"], RT + 2)
            pe.wait_ge(S["bounds_made"], 1)
            pe.transpose(PS[0:2 * RT, 0, 0:GROUPS], GB[:, 40:60], IDF[0:GROUPS, 0:GROUPS]).then_inc(S["bounds_t"], 1)
            pe.wait_ge(S["lim_row"], 1)
            pe.transpose(PS[0:1, 1, 0:2 * RT], LIMR[:, 0:1], IDF[0:2 * RT, 0:2 * RT]).then_inc(S["lim_t"], 1)
            pe.wait_ge(S["lim_made"], 1)
            cnt = pe.alloc_register("p_groups")
            pe.reg_mov(cnt, 0)

            def count_edges(b, j):
                lo, hi = block_bounds(pe, b)
                pe.wait_ge(S["inv_made"], b + 1)
                pe.matmul(PS[0:ROWS, 4 + j, 0:REL], ZERO[:, 0:ROWS], ZERO[:, 0:REL], start=True, stop=False)
                with pe.Fori(lo, hi) as e:
                    n = pe.snap(cnt, min_val=0, max_val=1 << 20)
                    slot = pe.snap((n % RING) * GRP, min_val=0, max_val=(RING - 1) * GRP)
                    first = pe.snap(e * GRP, min_val=0, max_val=TILES - GRP)
                    hot, types = HOTC[:, bass.ds(slot, GRP), :], TYPEHOT[:, bass.ds(first, GRP), :]
                    pe.wait_ge(S["hot1_made"], n + 1)
                    for k in range(GRP):
                        ins = pe.matmul(PS[0:ROWS, 4 + j, 0:REL], hot[:, k, :], types[:, k, :], start=False, stop=False)
                    ins.then_inc(S["hot1_used"], 1)
                    pe.reg_add(cnt, cnt, 1)
                pe.matmul(PS[0:ROWS, 4 + j, 0:REL], ZERO[:, 0:ROWS], ZERO[:, 0:REL], start=False, stop=True).then_inc(S["cnt_done"], 1)

            def row_products(X, t, slot, b0, done):
                for k in range(KT):
                    for xp, wps in ((0, (0, 1)), (1, (0,))):
                        for wp in wps:
                            for h in range(2):
                                ins = pe.matmul(PS[0:ROWS, b0 + h, 0:HALF], X[:, xp, k, bass.ts(t, ROWS)],
                                                WHL[:, bass.ds(slot, 1), wp, k * D + h * HALF:k * D + (h + 1) * HALF].rearrange("p a c -> p (a c)"),
                                                start=k == 0 and xp + wp == 0, stop=k == KT - 1 and xp == 1)
                ins.then_inc(done, 1)

            def full_products(t, W, b0, done):
                for k in range(KT):
                    for h in range(2):
                        ins = pe.matmul(PS[0:ROWS, b0 + h, 0:HALF], HF[:, k, t * ROWS:(t + 1) * ROWS],
                                        W[:, k * D + h * HALF:k * D + (h + 1) * HALF], start=k == 0, stop=k == KT - 1)
                ins.then_inc(done, 1)

            for L in range(2):
                X = XT if L == 0 else HT
                if L == 1:
                    pe.wait_ge(S["h_free"], RT + 2)

                def panel(p, counts):
                    pe.wait_ge(S["w_lo"], p + ((REL + 1) * L + 1))
                    pe.sem_inc(S["pe_tick"], 1)
                    slot = (p + L) % 2
                    with pe.Fori(0, RT // 2) as i:
                        for j in range(2):
                            t = i * 2 + j
                            pe.wait_ge(S["pair_out"], p * RT + t + (100 * L + 1))
                            row_products(X, t, slot, 2 * j, S["acc_done"])
                            if counts:
                                count_edges(t, j)

                if L == 0:
                    panel(0, True)
                    pe.reg_mov(cnt, 0)
                with pe.Fori(1 - L, REL + 1) as p:
                    panel(p, False)

                def aggregate(b, j):
                    lo, hi = block_bounds(pe, b)
                    pe.wait_ge(S["pair_out"], b + (100 * L + 90 + 1))
                    for h in range(2):
                        pe.matmul(PS[0:ROWS, 2 * j + h, 0:HALF], ZERO[:, 0:ROWS], ZERO[:], start=True, stop=False)
                    with pe.Fori(lo, hi) as e:
                        n = pe.snap(cnt, min_val=0, max_val=1 << 20)
                        for k in range(GRP):
                            pe.wait_ge(S["hot_made"], n * GRP + (k + 1))
                            pe.wait_ge(S[f"gat_in{k}"], n * 16 + 16)
                            for h in range(2):
                                ins = pe.matmul(PS[0:ROWS, 2 * j + h, 0:HALF], HOT[:, k, :], GAT[:, k, h * HALF:(h + 1) * HALF],
                                                start=False, stop=False)
                            ins.then_inc(S["edge_used"], 1)
                        pe.reg_add(cnt, cnt, 1)
                    for h in range(2):
                        ins = pe.matmul(PS[0:ROWS, 2 * j + h, 0:HALF], ZERO[:, 0:ROWS], ZERO[:], start=False, stop=True)
                    ins.then_inc(S["acc_done"], 1)

                def transpose_h(b, j):
                    if L == 0:
                        pe.wait_ge(S["relu_made"], b + 1)
                        pe.wait_ge(S["h_free"], b + 1)
                        six_transposes(4 + 2 * j, 2 + j, S["h_t"])

                aggregate(0, 0)
                aggregate(1, 1)
                with pe.Fori(0, RT // 2 - 1) as i:
                    for j in range(2):
                        aggregate(i * 2 + (2 + j), j)
                        transpose_h(i * 2 + j, j)
                transpose_h(RT - 2, 0)
                transpose_h(RT - 1, 1)
            pe.wait_ge(S["pair_out"], 200 + 2)
            pe.wait_ge(S["ones_made"], 1)
            pe.wait_ge(S["rf_in"], 16)
            with pe.Fori(0, PAIRS) as it:
                slot = it % 2
                pe.wait_ge(S["w_lo"], it + (W_MIX + 1))
                pe.sem_inc(S["pe_tick"], 1)

                def w(part, k, x):
                    return WHM[:, bass.ds(slot, 1), part, (k * 3 + x) * 128:(k * 3 + x + 1) * 128].rearrange("p a c -> p (a c)")

                for x, nm in ((0, "q"), (1, "k")):
                    for c, (c0, n) in enumerate(CHUNKS):
                        mix.wait_banks(pe, it, f"{nm}{c}")
                        for k in range(KT):
                            for wp, xp in ((0, 0), (0, 1), (1, 0)):
                                ins = pe.matmul(PS[:, mix.bank(f"{nm}{c}"), 0:n], w(wp, k, x), XT[:, xp, k, c0:c0 + n],
                                                start=k == 0 and wp + xp == 0, stop=k == KT - 1 and wp == 1)
                        ins.then_inc(S["mix_pe"], 1)
                for c in range(3):
                    mix.wait_banks(pe, it, f"v{c}")
                    for t in range(4 * c, min(4 * c + 4, RT)):
                        for k in range(KT):
                            for xp, wp in ((0, 0), (0, 1), (1, 0)):
                                ins = pe.matmul(PS[0:ROWS, mix.bank(f"v{c}"), (t % 4) * 128:(t % 4) * 128 + 128],
                                                XT[:, xp, k, t * ROWS:(t + 1) * ROWS], w(wp, k, 2),
                                                start=k == 0 and wp + xp == 0, stop=k == KT - 1 and xp == 1)
                    ins.then_inc(S["mix_pe"], 1)
                def outputs(h):
                    pe.wait_ge(S["mix_dve"], mix.taken(it, f"kv{h}"))
                    pe.wait_ge(S["mix_act"], mix.taken(it, f"Q{h}12"))
                    for c, (c0, n) in enumerate(CHUNKS):
                        mix.wait_banks(pe, it, f"o{h}{c}")
                        for m in range(2):
                            ins = pe.matmul(PS[:, mix.bank(f"o{h}{c}"), 0:n], KV[:, m, :], QP[:, m, c0:c0 + n], start=m == 0, stop=m == 1)
                        ins.then_inc(S["mix_pe"], 1)

                for h in range(2):
                    if h == 0:
                        pe.wait_ge(S["mix_act"], mix.taken(it, "k2"))
                    for u in range(RT // 2):
                        mix.wait_banks(pe, it, f"K{h}{u}")
                        for t in (2 * u, 2 * u + 1):
                            ins = pe.matmul(PS[0:ROWS, mix.bank(f"K{h}{u}"), (t % 2) * MF:(t % 2 + 1) * MF],
                                            KA[:, h, t * ROWS:(t + 1) * ROWS], RF[:, h, :], start=True, stop=True)
                        ins.then_inc(S["mix_pe"], 1)
                    if h == 1:
                        outputs(0)
                    for m in range(2):
                        for c, (c0, n) in enumerate(CHUNKS):
                            mix.wait_banks(pe, it, f"Q{h}{m}{c}")
                            pe.matmul(PS[:, mix.bank(f"Q{h}{m}{c}"), 0:n], RF[:, h, m * 128:(m + 1) * 128], QA[:, h, c0:c0 + n],
                                      start=True, stop=True).then_inc(S["mix_pe"], 1)
                    mix.wait_banks(pe, it, f"kv{h}")
                    pe.wait_ge(S["mix_act"], mix.taken(it, f"K{h}4"))
                    pe.wait_ge(S["mix_dve"], mix.taken(it, "v2"))
                    for m in range(2):
                        for t in range(RT):
                            ins = pe.matmul(PS[:, mix.bank(f"kv{h}"), m * 128:(m + 1) * 128], KP[:, t, m * 128:(m + 1) * 128],
                                            VA[:, t, h, :], start=t == 0, stop=t == RT - 1)
                    ins.then_inc(S["mix_pe"], 1)
                outputs(1)
            pe.wait_ge(S["hf_made"], PAIRS)
            pe.wait_ge(S["wp_in"], 16)
            for i in range(RT // 2):
                for t in range(*((0, 4) if i == 0 else (2 * i + 2, min(2 * i + 4, RT)))):
                    pe.wait_ge(S["mp_free"], t + 1)
                    full_products(t, WPR, 2 * (t % 2), S["mp_done"])
                for j in range(2):
                    t = i * 2 + j
                    pe.wait_ge(S["xf_made"], t + 1)
                    pe.wait_ge(S["xf_free"], t + 1)
                    six_transposes(4 + 2 * j, 2 + j, S["xf_t"])
            pe.wait_ge(S["w_lo"], W_LORA + 1)
            pe.wait_ge(S["xf_free"], RT + 2)
            pe.wait_ge(S["mp_free"], RT + 2)
            with pe.Fori(0, RT // 2) as i:
                for j in range(2):
                    t = i * 2 + j
                    pe.wait_ge(S["lg_free"], t + 1)
                    for k in range(KT):
                        for xp, wp in ((0, 0), (0, 1), (1, 0)):
                            ins = pe.matmul(PS[0:ROWS, j, 0:LW + EXPERTS], XT[:, xp, k, bass.ts(t, ROWS)],
                                            WHM[:, W_LORA % 2, wp, k * (LW + EXPERTS):(k + 1) * (LW + EXPERTS)],
                                            start=k == 0 and xp + wp == 0, stop=k == KT - 1 and xp == 1)
                    ins.then_inc(S["lg_pe"], 1)
            pe.wait_ge(S["gate_done"], 1)
            for u in range(RT // 2):
                for k in range(2):
                    for t in range(2):
                        ins = pe.transpose(PS[:, 2 + u, (2 * k + t) * ROWS:(2 * k + t + 1) * ROWS],
                                           HG[:, 2 * u + t, k * 128:(k + 1) * 128], IDF[0:ROWS, 0:ROWS])
                ins.then_inc(S["lt_pe"], 1)
            pe.wait_ge(S["lt_free"], RT // 2)
            pe.wait_ge(S["ffn_ready"], 1)
            with pe.Fori(0, PAIRS) as it:
                pe.wait_ge(S["w_lo"], it + (W_FFN + 1))
                pe.sem_inc(S["pe_tick"], 1)
                slot = (it + W_FFN) % 2

                def wf(part, k, x):
                    return WHM[:, bass.ds(slot, 1), part, (k * 3 + x) * 128:(k * 3 + x + 1) * 128].rearrange("p a c -> p (a c)")

                def ranks(k, x):
                    return F67[:, (k * 3 + x) * 128:(k * 3 + x + 1) * 128]

                for x, nm in ((0, "q"), (1, "k")):
                    for c, (c0, n) in enumerate(CHUNKS):
                        ffn.wait_banks(pe, it, f"{nm}{c}")
                        for k in range(KT):
                            for wp, xp in ((0, 0), (0, 1), (1, 0)):
                                pe.matmul(PS[:, ffn.bank(f"{nm}{c}"), 0:n], wf(wp, k, x), XT[:, xp, k, c0:c0 + n],
                                          start=k == 0 and wp + xp == 0, stop=False)
                        for k in range(2):
                            ins = pe.matmul(PS[:, ffn.bank(f"{nm}{c}"), 0:n], ranks(k, x), LT[:, k, c0:c0 + n], start=False, stop=k == 1)
                        ins.then_inc(S["ffn_pe"], 1)
                for r, e, _ in FFN:
                    if r[0] in "qkvO":
                        continue
                    if r[0] == "W":
                        t = int(r[1])
                        if t % 4 == 0:
                            ffn.wait_banks(pe, it, f"v{t // 4}")
                        o = PS[0:ROWS, ffn.bank(f"v{t // 4}"), (t % 4) * 128:(t % 4) * 128 + 128]
                        for k in range(KT):
                            for xp, wp in ((0, 0), (0, 1), (1, 0)):
                                pe.matmul(o, XT[:, xp, k, t * ROWS:(t + 1) * ROWS], wf(wp, k, 2), start=k == 0 and wp + xp == 0, stop=False)
                        for k in range(2):
                            ins = pe.matmul(o, LT[:, k, t * ROWS:(t + 1) * ROWS], ranks(k, 2), start=False, stop=k == 1)
                        if t % 4 == 3 or t == RT - 1:
                            ins.then_inc(S["ffn_pe"], 1)
                        continue
                    h = int(r[1])
                    half = slice(64 * h, 64 * h + 64)
                    if r[0] == "M":
                        s_ = int(r[2])
                        if r == "M00":
                            pe.wait_ge(S["ffn_dve"], ffn.taken(it, "k2"))
                        ffn.wait_banks(pe, it, r)
                        for b in range(3):
                            n = min(512, N - 512 * b)
                            ins = pe.matmul(PS[0:ROWS, ffn.bank(r) + b, 0:n], QS[:, h, s_ * ROWS:(s_ + 1) * ROWS], KS[:, h, 512 * b:512 * b + n],
                                            start=True, stop=True)
                        ins.then_inc(S["ffn_pe"], 1)
                    elif r[0] == "S":
                        c, t = int(r[2]), int(r[3])
                        c0, n = CHUNKS[c]
                        if t == 0:
                            pe.wait_ge(S[f"dg{h}_made"], it * RT + min(4 * c + 4, RT))
                        ffn.wait_banks(pe, it, r)
                        p = PS[0:ROWS, ffn.bank(r), 0:n]
                        pe.matmul(p, KS[:, h, t * ROWS:(t + 1) * ROWS], QS[:, h, c0:c0 + n], start=True, stop=False)
                        pe.matmul(p, KS[half, h, t * ROWS:(t + 1) * ROWS], QL[half, c0:c0 + n], start=False, stop=False)
                        pe.matmul(p, ONB[0:ROWS, 0:ROWS], DG[:, h, c0:c0 + n], start=False, stop=True).then_inc(S["ffn_pe"], 1)
                    else:
                        c, t = int(r[2]), int(r[3])
                        n, k = CHUNKS[c][1], h * 30 + c * 10 + t
                        if t == 0:
                            ffn.wait_banks(pe, it, f"O{h}{c}")
                            if h == 0 and c == 0:
                                pe.wait_ge(S["ffn_dve"], ffn.taken(it, "v2"))
                        pe.wait_ge(S["ffn_lo"], it * 60 + (k + 1 + EXPS))
                        o = PS[:, ffn.bank(f"O{h}{c}"), 0:n]
                        for vp, pp in ((0, 0), (0, 1), (1, 0)):
                            ins = pe.matmul(o, V2[:, vp, t, h, :], P2[:, k % PARTED, pp, 0:n], start=t == 0 and vp + pp == 0, stop=t == RT - 1 and vp == 1)
                        if t == RT - 1:
                            ins.then_inc(S["ffn_pe"], 1)
                            pe.drain().then_inc(S["av_done"], 1)
                        else:
                            ins.then_inc(S["av_done"], 1)
            pe.wait_ge(S["wp_in"], 32)
            pe.wait_ge(S["ffn_dve"], ffn.taken(PAIRS - 1, "O12"))
            for i in range(RT // 2):
                for j in range(2):
                    pe.wait_ge(S["fp_free"], i * 2 + (j + 1))
                    full_products(i * 2 + j, WST, 2 * j, S["fp_done"])


def lay_out(np, inp):
    a = {k: np.asarray(v) for k, v in inp.items()}
    pad = TILES * 128 - E

    def edges(v, fill):
        return np.concatenate([v, np.full(pad, fill, v.dtype)])

    def slices(w):
        return w.reshape(-1, 128, w.shape[1]).transpose(1, 0, 2)

    o = {"x": a["x"], "ident": np.eye(128, dtype=np.float32)}
    for name, key, fill in (("srcT", "src", 0), ("dstT", "dst", PAD_DST), ("etT", "edge_type_8", 0)):
        o[name] = np.ascontiguousarray(edges(a[key], fill).reshape(TILES, 128).T)
    o["dstG"] = edges(a["dst"], PAD_DST).reshape(GROUPS, GRP * 128)
    cst = np.zeros((128, 160), np.float32)
    cst[:, 0:128] = np.arange(128)
    cst[:, 128:138] = ROWS * np.arange(RT)
    cst[:, 138:148] = ROWS * (np.arange(RT) + 1)
    cst[:, 148] = np.arange(128) + 1
    cst[:, 149] = GROUPS - np.arange(128)
    o["cst"] = cst
    o["wg"] = np.concatenate([slices(w).reshape(128, KT * D) for l in "12"
                              for w in [*a[f"L0_gnn_W{l}"], a[f"L0_gnn_root{l}"]]])
    o["b1"], o["b2"] = a["L0_gnn_b1"].reshape(1, D), a["L0_gnn_b2"].reshape(1, D)
    wqkv = a["L0_mix_W_qkv"].reshape(KT, 128, 3, PAIRS, 128)
    o["wm"] = np.ascontiguousarray(wqkv.transpose(3, 1, 0, 2, 4)).reshape(PAIRS * 128, WM)
    rft, half = a["L0_mix_random_features"].T, np.full((DH, MF), -0.5, np.float32)
    o["rf"] = np.concatenate([np.concatenate([rft, half]), np.concatenate([half, rft])], axis=1)
    o["wmp"] = slices(a["L0_mix_W_proj"]).reshape(128, KT * D)
    o["bmp"], o["gamma"], o["beta"] = (a[f"L0_mix_{n}"].reshape(1, D) for n in ("b_proj", "gamma", "beta"))
    wa = slices(np.concatenate([a["L0_ffn_A"].reshape(LW, D), a["L0_ffn_Wg"]]).T).reshape(128, -1)
    o["wa"] = np.concatenate([wa, np.zeros((128, WM - wa.shape[1]), np.float32)], axis=1)
    o["bag"] = np.concatenate([a["L0_ffn_ba"].reshape(LW), a["L0_ffn_bg"]])[None]
    o["tri"] = np.tile(np.tril(np.ones((EXPERTS, EXPERTS), np.float32), -1).reshape(1, -1), (128, 1))
    wf = np.concatenate([a["L0_ffn_Wqkv"].T, a["L0_ffn_Bm"].transpose(0, 2, 1).reshape(LW, 3 * D), a["L0_ffn_bb"],
                         a["L0_ffn_bqkv"][None], np.zeros((128 - EXPERTS - 1, 3 * D), np.float32)])
    o["wf"] = np.ascontiguousarray(wf.reshape(KF, 128, 3, PAIRS, 128).transpose(3, 1, 0, 2, 4)).reshape(PAIRS * 128, WF)
    o["wo"] = slices(a["L0_ffn_Wproj"].T).reshape(128, KT * D)
    o["bo"] = a["L0_ffn_bproj"].reshape(1, D)
    return {k: np.ascontiguousarray(v) for k, v in o.items()}


def kernel(**inputs):
    import numpy as _np
    import concourse.bacc as _bacc
    from concourse import mybir as _mybir
    from concourse.bass_utils import run_bass_kernel_spmd as _run

    nc = _bacc.Bacc("TRN2", target_bir_lowering=False, num_devices=1)
    arrays, a = {}, {}
    for name, v in lay_out(_np, inputs).items():
        arrays[f"in_{name}_dram"] = v
        a[name] = nc.dram_tensor(f"in_{name}_dram", v.shape, _mybir.dt.from_np(v.dtype), kind="ExternalInput").ap()
    out = nc.dram_tensor("out_0_dram", (N, D), _mybir.dt.float32, kind="ExternalOutput").ap()
    graph_and_attentions_kernel(nc, a, out)
    r = _run(nc, [arrays], core_ids=[0])
    return r.results[0]["out_0_dram"]
```
